# Optimizing a Trainium2 kernel written in Bass

```python
import numpy as np
import jax
import jax.numpy as jnp

def _softmax(x, axis=-1):
    return jax.nn.softmax(x, axis=axis)

def _gelu(x):
    return jax.nn.gelu(x, approximate=True)

def _silu(x):
    return jax.nn.silu(x)

def _sigmoid(x):
    return jax.nn.sigmoid(x)

def _layernorm(x, axis=-1, eps=1e-05):
    m = jnp.mean(x, axis=axis, keepdims=True)
    v = jnp.var(x, axis=axis, keepdims=True)
    return (x - m) / jnp.sqrt(v + eps)

def _scatter_add(tgt, idx, src, axis=0):
    return tgt.at[idx].add(src)

def _segment_sum(src, seg, n):
    return jax.ops.segment_sum(src, seg, n)
kernel_name = 'mk_xattn_seq_d2_seqx_r4_70fc4a'

def setup_inputs(seed: int=0):
    np.random.seed(seed)
    _w = jnp.asarray

    def _rec_inputs():
        import jax
        import jax.numpy as jnp
        _rk = jax.random.key(seed)
        x = -0.0003929 + 0.9999 * jax.random.normal(jax.random.fold_in(_rk, 1), (32, 256, 256), jnp.float32)
        _lenS = 256 - jax.random.randint(jax.random.fold_in(_rk, 7), (32,), 0, max(1, 256 // 4) + 1, jnp.int32)
        _lenS2 = 120 - jax.random.randint(jax.random.fold_in(_rk, 8), (32,), 0, max(1, 120 // 4) + 1, jnp.int32)
        _ctx_1024P = jax.random.normal(jax.random.fold_in(_rk, 11), (32, 16, 256), jnp.float32)
        _ctx_1024c = jax.random.dirichlet(jax.random.fold_in(_rk, 511), 0.3 * jnp.ones((16,), jnp.float32), (32, 120))
        _ctx_1024t = jnp.einsum('bsk,bkd->bsd', _ctx_1024c, _ctx_1024P)
        _ctx_1024t = _ctx_1024t * jax.lax.rsqrt(jnp.mean(jnp.square(_ctx_1024t)) + 1e-12) * 0.953939
        ctx_1024 = 0.000227908 + 0.99994 * (_ctx_1024t + 0.3 * jax.random.normal(jax.random.fold_in(_rk, 611), (32, 120, 256), jnp.float32))
        itok_BxS_0_255 = jax.random.randint(jax.random.fold_in(_rk, 12), (32, 256), 0, 64, jnp.int32)
        return (x, ctx_1024, itok_BxS_0_255)
    x, ctx_1024, itok_BxS_0_255 = _rec_inputs()

    def _L0_xattn_setup():
        import jax, jax.numpy as jnp
        import numpy as np
        import math
        EPS_RMS = 1.1920929e-07
        EPS_DEN = 1e-06

        def rmsnorm(x, gamma):
            ms = jnp.mean(x * x, axis=-1, keepdims=True)
            return x * jax.lax.rsqrt(ms + EPS_RMS) * gamma
        key = jax.random.key(seed)
        ks = jax.random.split(key, 8)
        B, T, K, D = (4, 1024, 64, 256)
        x_tokens = jax.random.normal(ks[0], (B, T, D), dtype=jnp.float32)
        ctx = jax.random.normal(ks[1], (B, K, D), dtype=jnp.float32)
        idx = jnp.sort(jax.random.randint(ks[2], (B, T), 0, K), axis=-1)
        s = 1.0 / math.sqrt(D)
        Wq = jax.random.normal(ks[3], (D, D), dtype=jnp.float32) * s
        Wk = jax.random.normal(ks[4], (D, D), dtype=jnp.float32) * s
        Wv = jax.random.normal(ks[5], (D, D), dtype=jnp.float32) * s
        Wo = jax.random.normal(ks[6], (D, D), dtype=jnp.float32) * s
        return {'x_tokens': x_tokens, 'ctx': ctx, 'ctx_index_per_token': idx, 'gamma_q': jnp.ones((D,), jnp.float32), 'gamma_kv': jnp.ones((D,), jnp.float32), 'Wq': Wq, 'Wk': Wk, 'Wv': Wv, 'Wo': Wo}
    _L0_xattn_all = _L0_xattn_setup()
    _L0_xattn_in = {k: v for k, v in _L0_xattn_all.items() if k in ('gamma_q', 'gamma_kv', 'Wq', 'Wk', 'Wv', 'Wo')}
    del _L0_xattn_all

    def _L1_xattn_setup():
        import jax, jax.numpy as jnp
        import numpy as np
        B, Q, KV = (2, 512, 512)
        D_MODEL = 256
        N_HEADS = 16
        D_KV = 64
        EPS = 1e-06
        key = jax.random.key(seed)
        ks = jax.random.split(key, 7)
        s = 0.02
        return {'hidden_states': jax.random.normal(ks[0], (B, Q, D_MODEL), jnp.float32), 'key_value_states': jax.random.normal(ks[1], (B, KV, D_MODEL), jnp.float32), 'wq': jax.random.normal(ks[2], (D_MODEL, N_HEADS * D_KV), jnp.float32) * s, 'wk': jax.random.normal(ks[3], (D_MODEL, N_HEADS * D_KV), jnp.float32) * s, 'wv': jax.random.normal(ks[4], (D_MODEL, N_HEADS * D_KV), jnp.float32) * s, 'wo': jax.random.normal(ks[5], (N_HEADS * D_KV, D_MODEL), jnp.float32) * s, 'norm_w': jnp.ones((D_MODEL,), jnp.float32)}
    _L1_xattn_all = _L1_xattn_setup()
    _L1_xattn_in = {k: v for k, v in _L1_xattn_all.items() if k in ('wq', 'wk', 'wv', 'wo', 'norm_w')}
    del _L1_xattn_all
    return {'x': x, 'ctx_1024': ctx_1024, 'itok_BxS_0_255': itok_BxS_0_255, 'L0_xattn_gamma_q': _L0_xattn_in['gamma_q'], 'L0_xattn_gamma_kv': _L0_xattn_in['gamma_kv'], 'L0_xattn_Wq': _L0_xattn_in['Wq'], 'L0_xattn_Wk': _L0_xattn_in['Wk'], 'L0_xattn_Wv': _L0_xattn_in['Wv'], 'L0_xattn_Wo': _L0_xattn_in['Wo'], 'L1_xattn_wq': _L1_xattn_in['wq'], 'L1_xattn_wk': _L1_xattn_in['wk'], 'L1_xattn_wv': _L1_xattn_in['wv'], 'L1_xattn_wo': _L1_xattn_in['wo'], 'L1_xattn_norm_w': _L1_xattn_in['norm_w']}

def reference(x, ctx_1024, itok_BxS_0_255, L0_xattn_gamma_q, L0_xattn_gamma_kv, L0_xattn_Wq, L0_xattn_Wk, L0_xattn_Wv, L0_xattn_Wo, L1_xattn_wq, L1_xattn_wk, L1_xattn_wv, L1_xattn_wo, L1_xattn_norm_w):
    import jax
    import jax.numpy as jnp

    def _L0_xattn_ref(x_tokens, ctx, ctx_index_per_token, gamma_q, gamma_kv, Wq, Wk, Wv, Wo):
        import jax, jax.numpy as jnp
        import numpy as np
        import math
        EPS_RMS = 1.1920929e-07
        EPS_DEN = 1e-06

        def rmsnorm(x, gamma):
            ms = jnp.mean(x * x, axis=-1, keepdims=True)
            return x * jax.lax.rsqrt(ms + EPS_RMS) * gamma
        B, T, D = x_tokens.shape
        K = ctx.shape[1]
        H = 16
        hd = D // H

        def split(x):
            return x.reshape(B, -1, H, hd).transpose(0, 2, 1, 3)
        q = split(rmsnorm(x_tokens, gamma_q) @ Wq.T)
        kn = rmsnorm(ctx, gamma_kv)
        k = split(kn @ Wk.T)
        v = split(kn @ Wv.T)
        ctx_pos = jnp.arange(K)[None, None, :]
        mask = (jnp.abs(ctx_pos - ctx_index_per_token[:, :, None]) <= 1)[:, None]
        scores = jnp.einsum('bhqd,bhkd->bhqk', q, k) / math.sqrt(hd)
        w = jnp.square(jax.nn.relu(scores))
        w = jnp.where(mask, w, 0.0)
        denom = jnp.maximum(w.sum(-1, keepdims=True), EPS_DEN)
        out = jnp.einsum('bhqk,bhkd->bhqd', w / denom, v)
        out = out.transpose(0, 2, 1, 3).reshape(B, T, D)
        return x_tokens + out @ Wo.T

    def _L1_xattn_ref(hidden_states, key_value_states, wq, wk, wv, wo, norm_w):
        import jax, jax.numpy as jnp
        import numpy as np
        B, Q, KV = (2, 512, 512)
        D_MODEL = 256
        N_HEADS = 16
        D_KV = 64
        EPS = 1e-06
        var = jnp.mean(jnp.square(hidden_states), axis=-1, keepdims=True)
        normed = hidden_states * jax.lax.rsqrt(var + EPS) * norm_w
        b, q_len, _ = hidden_states.shape
        kv_len = key_value_states.shape[1]

        def split_heads(x):
            return x.reshape(b, -1, N_HEADS, D_KV).transpose(0, 2, 1, 3)
        q = split_heads(normed @ wq)
        k = split_heads(key_value_states @ wk)
        v = split_heads(key_value_states @ wv)
        scores = jnp.einsum('bhqd,bhkd->bhqk', q, k)
        attn = jax.nn.softmax(scores.astype(jnp.float32), axis=-1).astype(scores.dtype)
        ctx = jnp.einsum('bhqk,bhkd->bhqd', attn, v)
        ctx = ctx.transpose(0, 2, 1, 3).reshape(b, q_len, N_HEADS * D_KV)
        attn_out = ctx @ wo
        return hidden_states + attn_out
    x = _L0_xattn_ref(x, ctx_1024, itok_BxS_0_255, L0_xattn_gamma_q, L0_xattn_gamma_kv, L0_xattn_Wq, L0_xattn_Wk, L0_xattn_Wv, L0_xattn_Wo)
    x = _L1_xattn_ref(x, ctx_1024, L1_xattn_wq, L1_xattn_wk, L1_xattn_wv, L1_xattn_wo, L1_xattn_norm_w)
    return x

_drawn_inputs = setup_inputs


def setup_inputs(seed=0):
    import zlib

    import numpy as np

    out = dict(_drawn_inputs(seed))
    spreads = {'L0_xattn_gamma_q': (1.0, 0.2),
     'L0_xattn_gamma_kv': (1.0, 0.2),
     'L1_xattn_norm_w': (1.0, 0.2)}
    factors = {}
    for name, (base, spread) in spreads.items():
        noise = np.random.default_rng([zlib.crc32(name.encode()), seed]).standard_normal(out[name].shape)
        drawn = base * np.exp(spread * noise) if base else spread * noise
        out[name] = jnp.asarray(drawn.astype(out[name].dtype))
    for name, factor in factors.items():
        out[name] = (out[name] * factor).astype(out[name].dtype)
    return out
```

```python
from contextlib import ExitStack

import concourse.bass as bass
from concourse import mybir
from concourse.alu_op_type import AluOpType as ALU

F32 = mybir.dt.float32
F32R = mybir.dt.float32r
I32 = mybir.dt.int32
ACT = mybir.ActivationFunctionType
X_AXIS = mybir.AxisListType.X

P = 128
NB, T, D = 32, 256, 256
CTX = 120
H0, HD0 = 16, 16
H1, HD1 = 16, 64
E1 = H1 * HD1
TT = T // P
DC = D // P
EC = E1 // P
NEIGH = 3
HG = 4
NHG = H1 // HG
NG = NHG * TT
GC = HG * CTX
LOADS = 5
ROOT = D ** -0.5
EPS0, EPS1, EPS_DEN = 1.1920929e-07, 1e-06, 1e-06

TURNS = [("q_1", -1, 0), ("w1", -2, 1), ("kv0", 0, 0), ("v_0", 0, 1), ("q_2", -1, 0), ("q_3", -1, 1),
         ("v_1", 0, 0), ("oT", 0, 1), ("oW", 0, 0), ("w0", -1, 1), ("xT", 0, 0), ("q_0", 0, 0)]
BANK = {name: bank for name, _, bank in TURNS}


def turn_before(name, s):
    at = [n for n, _, _ in TURNS].index(name)
    back = [(n, rel) for n, rel, _ in reversed(TURNS[:at])] + [(n, rel - 1) for n, rel, _ in reversed(TURNS)]
    for n, rel in back:
        if BANK[n] == BANK[name] and 0 <= s + rel < NB:
            return n, rel
    return None


def build(nc, x, xT, ctx, ctxT, idx, gammas, w0qT, w0kT, w0vT, w0oT, w1q, w1k, w1v, w1o, out):
    st = ExitStack()
    with st:
        def sb(name, shape, dt=F32):
            return st.enter_context(nc.sbuf_tensor(name, shape, dt))

        def ps(name, shape):
            return st.enter_context(nc.psum_tensor(name, shape, F32))

        def sem(name):
            return st.enter_context(nc.semaphore(name))

        w0q_hi, w0q_lo = sb("w0q_hi", [P, DC, D], F32R), sb("w0q_lo", [P, DC, D], F32R)
        w0kv_hi, w0kv_lo = sb("w0kv_hi", [P, DC, 2, D], F32R), sb("w0kv_lo", [P, DC, 2, D], F32R)
        w0o_hi, w0o_lo = sb("w0o_hi", [P, DC, D], F32R), sb("w0o_lo", [P, DC, D], F32R)
        w1q_hi, w1q_lo = sb("w1q_hi", [P, DC, E1], F32R), sb("w1q_lo", [P, DC, E1], F32R)
        w1v_hi, w1v_lo = sb("w1v_hi", [P, DC, E1], F32R), sb("w1v_lo", [P, DC, E1], F32R)
        w1o_hi, w1o_lo = sb("w1o_hi", [P, EC, D], F32R), sb("w1o_lo", [P, EC, D], F32R)
        w1k_sb = sb("w1k_sb", [P, DC, E1])
        gamma = sb("gamma", [P, 3, DC])
        ident = sb("ident", [P, P])
        pos_i = sb("pos_i", [P, NEIGH], I32)
        pos = sb("pos", [P, NEIGH])
        small_consts = sb("small_consts", [P, 8])
        eps0, eps1 = small_consts[:, 0:3], small_consts[:, 3:5]
        half = small_consts[:, 5:8]
        x_in = [sb(f"x_in{u}", [P, TT, D]) for u in range(2)]
        xT_in = [sb(f"xT_in{u}", [P, DC, T]) for u in range(2)]
        ctx_in = [sb(f"ctx_in{u}", [CTX, D]) for u in range(2)]
        ctxT_in = [sb(f"ctxT_in{u}", [P, DC, CTX]) for u in range(2)]
        idx_in = [sb(f"idx_in{u}", [CTX, T], I32) for u in range(2)]
        junk = sb("junk", [P, 5, D], mybir.dt.bfloat16)
        ms = [sb(f"ms_{u}", [P, 3]) for u in range(2)]
        ms_eps = sb("ms_eps", [P, 3])
        rs = [sb(f"rs_{u}", [P, 3]) for u in range(2)]
        xT_hi, xT_lo = sb("xT_hi", [P, DC, T], F32R), sb("xT_lo", [P, DC, T], F32R)
        cT_hi, cT_lo = sb("cT_hi", [P, DC, CTX], F32R), sb("cT_lo", [P, DC, CTX], F32R)
        onehot = sb("onehot", [CTX, NEIGH, T], F32R)
        q0 = sb("q0", [P, TT, D])
        kv_hi, kv_lo = sb("kv_hi", [CTX, 2, D], F32R), sb("kv_lo", [CTX, 2, D], F32R)
        prod = sb("prod", [P, NEIGH * D])
        s0 = sb("s0", [P, TT, NEIGH, H0])
        w0 = sb("w0", [P, TT, NEIGH, H0])
        den = sb("den", [P, TT, H0])
        den_c = sb("den_c", [P, TT, H0])
        rden = sb("rden", [P, TT, H0])
        wn = sb("wn", [P, TT, NEIGH, H0])
        o01 = sb("o01", [P, D])
        o0 = sb("o0", [P, TT, D])
        x1 = [sb(f"x1_{u}", [P, TT, D]) for u in range(2)]
        ms1, ms1_eps, rs1 = sb("ms1", [P, TT]), sb("ms1_eps", [P, TT]), sb("rs1", [P, TT])
        x1n = o0
        x1T_hi, x1T_lo = sb("x1T_hi", [P, DC, T], F32R), sb("x1T_lo", [P, DC, T], F32R)
        oT_hi, oT_lo = x1T_hi, x1T_lo
        q_hi = [sb(f"q_hi{n}", [P, 2, T], F32R) for n in range(2)]
        q_lo = [sb(f"q_lo{n}", [P, 2, T], F32R) for n in range(2)]
        k_hi = [sb(f"k_hi{u}", [P, EC, 2 * CTX], F32R) for u in range(2)]
        k_lo = [sb(f"k_lo{u}", [P, EC, 2 * CTX], F32R) for u in range(2)]
        v_pad = [sb(f"v_pad{u}", [P, EC, 4, HD1]) for u in range(2)]
        neg_max = sb("neg_max", [P, 4, HG])
        sums = sb("sums", [P, 4, HG])
        rsum = sb("rsum", [P, 4, HG])
        probs = [sb(f"probs{n}", [P, HG, CTX]) for n in range(4)]
        pT = [sb(f"pT{n}", [CTX, HG, T]) for n in range(2)]
        c_hi, c_lo = sb("c_hi", [P, EC, T], F32R), sb("c_lo", [P, EC, T], F32R)
        y = sb("y", [P, TT, D])

        score_ps = [ps(f"score_ps{n}", [P, 512]) for n in range(2)]
        pT_ps = ps("pT_ps", [P, 512])
        c_ps = ps("c_ps", [P, 512])
        g_ps = ps("g_ps", [P, 1024])
        turn_ps = [ps(f"turn_ps{n}", [P, 512]) for n in range(2)]

        inputs_in = [sem(f"inputs_in{u}") for u in range(2)]
        y_out = sem("y_out")
        w1k_in, gamma_in = sem("w1k_in"), sem("gamma_in")
        stage_in = [sem(f"stage_in{n}") for n in range(2)]
        staged_hi, stage_split = sem("staged_hi"), sem("stage_split")
        gamma_scaled = sem("gamma_scaled")
        v_zeroed, k_zeroed = sem("v_zeroed"), sem("k_zeroed")
        const_steps, const_done, pos_done = sem("const_steps"), sem("const_done"), sem("pos_done")
        pe_q0, pe_kv0, pe_kg, pe_vg = sem("pe_q0"), sem("pe_kv0"), sem("pe_kg"), sem("pe_vg")
        pe_oT, pe_oW, pe_xT = sem("pe_oT"), sem("pe_oW"), sem("pe_xT")
        pe_k, pe_v, pe_q, pe_s = sem("pe_k"), sem("pe_v"), sem("pe_q"), sem("pe_s")
        pe_pT, pe_c, pe_w = sem("pe_pT"), sem("pe_c"), sem("pe_w")
        ms_done, q0_done, kv_hi_done, oT_hi_done = sem("ms_done"), sem("q0_done"), sem("kv_hi_done"), sem("oT_hi_done")
        ms1_done, x1n_done, x1T_hi_done = sem("ms1_done"), sem("x1n_done"), sem("x1T_hi_done")
        k_hi_done, v_done, q_hi_done = sem("k_hi_done"), sem("v_done"), sem("q_hi_done")
        exp_done, pT_done, c_hi_done = sem("exp_done"), sem("pT_done"), sem("c_hi_done")
        cT_hi_done, xT_hi_done, kv_done = sem("cT_hi_done"), sem("xT_hi_done"), sem("kv_done")
        kprod_done, score0_done, weight_steps, weights_done = sem("kprod_done"), sem("score0_done"), sem("weight_steps"), sem("weights_done")
        vprod_done, pair_sum_done, o0_done, oT_done = sem("vprod_done"), sem("pair_sum_done"), sem("o0_done"), sem("oT_done")
        x1_done, x1T_done, k_done, q_done = sem("x1_done"), sem("x1T_done"), sem("k_done"), sem("q_done")
        max_done, rsum_done = sem("max_done"), sem("rsum_done")
        c_done, y_done = sem("c_done"), sem("y_done")
        cT_done, xT_done, ms_eps_done, rs_done = sem("cT_done"), sem("xT_done"), sem("ms_eps_done"), sem("rs_done")
        onehot_done, ms1_eps_done, rs1_done, norm_done = sem("onehot_done"), sem("ms1_eps_done"), sem("rs1_done"), sem("norm_done")

        def wait(eng, s, per_batch, batch, n):
            value = batch * per_batch + n
            if not isinstance(value, int) or value > 0:
                eng.wait_ge(s, value)

        def wait_inputs(eng, batch, u):
            eng.wait_ge(inputs_in[u], (batch - u) * (LOADS * 8) + LOADS * 16)

        def slots(eng, slot):
            slot(0, 0, 0)
            slot(1, 1, 1)
            with eng.Fori(1, NB // 2 - 1) as pair:
                slot(pair * 2, 0, 2)
                slot(pair * 2 + 1, 1, 3)
            slot(NB - 2, 0, NB - 2)
            slot(NB - 1, 1, NB - 1)
            slot(NB, 0, NB)

        EMPTIED = {"kv0": (kv_done, 1, 1), "oT": (oT_done, 1, 1),
                   "oW": (x1_done, 1, 1), "xT": (x1T_done, 1, 1),
                   "w0": (y_done, 2, 1), "w1": (y_done, 2, 2),
                   "v_0": (v_done, 2, 1), "v_1": (v_done, 2, 2),
                   "q_0": (q_done, 4, 1), "q_1": (q_done, 4, 2), "q_2": (q_done, 4, 3), "q_3": (q_done, 4, 4)}

        stages = [v_pad[n][:, :, :, :].rearrange("p a b c -> p (a b c)") for n in range(2)]
        big = stages[0].rearrange("p (c n) -> p c n", c=DC)
        quarter = [stages[1][:, n * DC * D:(n + 1) * DC * D].rearrange("p (c n) -> p c n", c=DC) for n in range(4)]

        block = st.enter_context(nc.Block())

        @block.sync
        def _(sp):
            def load(batch, u):
                one = bass.ds(batch, 1)
                for dst, src in (
                    (xT_in[u][:, :, :], xT[one].rearrange("a (c p) t -> p (a c) t", p=P)),
                    (ctxT_in[u][:, :, :], ctxT[one].rearrange("a (c p) t -> p (a c) t", p=P)),
                    (x_in[u][:, :, :], x[one].rearrange("a (t p) d -> p (a t) d", p=P)),
                    (ctx_in[u][:, :], ctx[one].rearrange("a p d -> (a p) d")),
                    (idx_in[u][:, :], idx[one].to_broadcast([CTX, T])),
                ):
                    sp.dma_start(dst, src).then_inc(inputs_in[u], 16)

            sp.dma_start(gamma[:, :, :], gammas).then_inc(gamma_in, 16)
            for n, w in enumerate((w0qT, w0kT, w0vT, w0oT)):
                sp.dma_start(quarter[n], w.rearrange("(c p) n -> p c n", p=P)).then_inc(stage_in[1], 16)
            load(0, 0)
            sp.dma_start(big, w1q.rearrange("(c p) n -> p c n", p=P)).then_inc(stage_in[0], 16)
            sp.dma_start(w1k_sb[:, :, :], w1k.rearrange("(c p) n -> p c n", p=P)).then_inc(w1k_in, 16)
            sp.wait_ge(stage_split, 4)
            sp.dma_start(stages[1].rearrange("p (c n) -> p c n", c=DC), w1v.rearrange("(c p) n -> p c n", p=P)).then_inc(stage_in[1], 16)
            load(1, 1)
            sp.wait_ge(stage_split, 5)
            sp.dma_start(stages[0].rearrange("p (c n) -> p c n", c=EC), w1o.rearrange("(c p) n -> p c n", p=P)).then_inc(stage_in[0], 16)

            def store(batch):
                wait(sp, y_done, 2, batch, 2)
                sp.dma_start(out[bass.ds(batch, 1)].rearrange("a (t p) d -> p (a t) d", p=P),
                             y[:, :, :]).then_inc(y_out, 16)

            def slot(s, u, kind):
                if kind >= 2:
                    store(s - 2)
                if kind < NB - 2:
                    wait(sp, x1_done, 1, s, 1)
                    wait(sp, rs_done, 1, s, 1)
                    wait(sp, xT_done, 1, s, 1)
                    wait(sp, cT_done, 1, s, 1)
                    wait(sp, pe_k, 2, s, 2)
                    wait(sp, onehot_done, 1, s, 1)
                    load(s + 2, u)

            slots(sp, slot)
            store(NB - 1)
            sp.wait_ge(y_out, 16 * NB)

        @block.gpsimd
        def _(pool):
            pool.memset(ident[:, :], 0.0).then_inc(const_steps, 1)
            pool.iota(pos_i[:, :], [[-1, NEIGH]], base=1, channel_multiplier=1).then_inc(const_steps, 1)
            pool.memset(eps0[:, :], EPS0).then_inc(const_steps, 1)
            pool.memset(eps1[:, :], EPS1).then_inc(const_steps, 1)
            pool.memset(half[:, :], -0.5).then_inc(const_steps, 1)
            pool.wait_ge(const_steps, 5)
            pool.affine_select(out=ident[:, :], in_=ident[:, :], compare_op=ALU.not_equal, fill=1.0,
                               base=0, pattern=[[-1, P]], channel_multiplier=1).then_inc(const_done, 1)

            def split_ctxT(c, u):
                wait(pool, cT_hi_done, 1, c, 1)
                wait_inputs(pool, c, u)
                pool.tensor_tensor(cT_lo[:, :, :], ctxT_in[u][:, :, :], cT_hi[:, :, :].bitcast(F32),
                                   ALU.subtract).then_inc(cT_done, 1)

            def split_xT(c, u):
                wait(pool, xT_hi_done, 1, c, 1)
                wait_inputs(pool, c, u)
                pool.tensor_tensor(xT_lo[:, :, :], xT_in[u][:, :, :], xT_hi[:, :, :].bitcast(F32),
                                   ALU.subtract).then_inc(xT_done, 1)

            def root0(c, u):
                wait(pool, ms_done, 1, c, 1)
                pool.tensor_tensor(ms_eps[:, :], ms[u][:, :], eps0[:, :], ALU.add).then_inc(ms_eps_done, 1)
                wait(pool, ms_eps_done, 1, c, 1)
                pool.tensor_tensor(rs[u][:, :], ms_eps[:, :], half[:, 0:3], ALU.pow).then_inc(rs_done, 1)

            def one_hots(c, u):
                for j in range(NEIGH):
                    last = pool.tensor_scalar(onehot[:, j, :], idx_in[u][:, :], pos[0:CTX, j:j + 1], None, ALU.is_equal)
                last.then_inc(onehot_done, 1)

            def gathers_over(c):
                wait(pool, pe_vg, 2, c, 2)

            def root1(c):
                wait(pool, ms1_done, 1, c, 1)
                pool.tensor_tensor(ms1_eps[:, :], ms1[:, :], eps1[:, :], ALU.add).then_inc(ms1_eps_done, 1)
                wait(pool, ms1_eps_done, 1, c, 1)
                pool.tensor_tensor(rs1[:, :], ms1_eps[:, :], half[:, 0:2], ALU.pow).then_inc(rs1_done, 1)

            def normalise(b, g):
                wait(pool, rsum_done, NG, b, g + 1)
                p = probs[g % 4][:, :, :]
                pool.tensor_tensor(p, p, rsum[:, g % 4, :].unsqueeze(2).broadcast_to([P, HG, CTX]),
                                   ALU.mult).then_inc(norm_done, 1)

            pool.wait_ge(pos_done, 1)
            split_xT(0, 0)
            split_ctxT(0, 0)
            root0(0, 0)
            one_hots(0, 0)

            def slot(s, u, kind):
                front, back, more = kind < NB, kind >= 1, kind < NB - 1
                b = s - 1
                if back:
                    normalise(b, 0)
                    normalise(b, 1)
                if more:
                    root0(s + 1, 1 - u)
                if back:
                    for g in range(2, 5):
                        normalise(b, g)
                if more:
                    gathers_over(s)
                if back:
                    normalise(b, 5)
                if more:
                    one_hots(s + 1, 1 - u)
                if back:
                    normalise(b, 6)
                    normalise(b, 7)
                if front:
                    root1(s)
                if more:
                    split_xT(s + 1, 1 - u)
                    split_ctxT(s + 1, 1 - u)

            slots(pool, slot)

        @block.scalar
        def _(act):
            def squares(c, u):
                wait_inputs(act, c, u)
                wait(act, rs_done, 1, c, 0)
                for t in range(TT):
                    act.activation(junk[:, t, :], x_in[u][:, t, :], ACT.Square, scale=ROOT, accum_out=ms[u][:, t:t + 1])
                act.activation(junk[0:CTX, 2, :], ctx_in[u][:, :], ACT.Square, scale=ROOT,
                               accum_out=ms[u][0:CTX, 2:3]).then_inc(ms_done, 1)

            def layer0_q(c, u):
                wait(act, pe_q0, 1, c, 1)
                wait(act, rs_done, 1, c, 1)
                wait(act, kprod_done, 2, c, 0)
                for t in range(TT):
                    last = act.activation(q0[:, t, :], g_ps[:, t * D:(t + 1) * D], ACT.Copy,
                                          scale=rs[u][:, t:t + 1])
                last.then_inc(q0_done, 1)

            def kv_high(c, u):
                wait(act, pe_kv0, 1, c, 1)
                wait(act, rs_done, 1, c, 1)
                wait(act, pe_vg, 2, c, 0)
                act.activation(kv_hi[:, :, :].rearrange("p a n -> p (a n)"), turn_ps[BANK["kv0"]][0:CTX, :], ACT.Copy,
                               scale=rs[u][0:CTX, 2:3]).then_inc(kv_hi_done, 1)

            def out_high(c):
                wait(act, pe_oT, 1, c, 1)
                wait(act, pe_q, 4, c - 1, 4)
                act.activation(oT_hi[:, :, :].rearrange("p a n -> p (a n)"), turn_ps[BANK["oT"]][:, :],
                               ACT.Copy).then_inc(oT_hi_done, 1)

            def squares1(c, u):
                wait(act, x1_done, 1, c, 1)
                wait(act, rs1_done, 1, c, 0)
                for t in range(TT):
                    last = act.activation(junk[:, 3 + t, :], x1[u][:, t, :], ACT.Square, scale=ROOT, accum_out=ms1[:, t:t + 1])
                last.then_inc(ms1_done, 1)

            def normed1(c, u):
                wait(act, rs1_done, 1, c, 1)
                wait(act, pe_oT, 1, c, 1)
                for t in range(TT):
                    last = act.activation(x1n[:, t, :], x1[u][:, t, :], ACT.Copy, scale=rs1[:, t:t + 1])
                last.then_inc(x1n_done, 1)

            def x1T_high(c):
                wait(act, pe_xT, 1, c, 1)
                wait(act, pe_oW, 1, c, 1)
                act.activation(x1T_hi[:, :, :].rearrange("p a n -> p (a n)"), turn_ps[BANK["xT"]][:, :],
                               ACT.Copy).then_inc(x1T_hi_done, 1)

            def k_high(c, u, k):
                wait(act, pe_k, 2, c, k + 1)
                wait(act, pe_s, NG, c - 1, 0)
                src = g_ps[:, k * 512:k * 512 + 4 * CTX].rearrange("p (c n) -> p c n", c=4)
                for h in range(2):
                    rows = slice(h * HD1, (h + 1) * HD1)
                    last = act.activation(k_hi[u][rows, 4 * k:4 * k + 4, h * CTX:(h + 1) * CTX], src[rows], ACT.Copy)
                last.then_inc(k_hi_done, 1)

            def v_copy(c, u, k):
                wait(act, pe_v, 2, c, k + 1)
                wait(act, pe_c, NHG, c - 1, 0)
                src = turn_ps[BANK[f"v_{k}"]][0:CTX, :].rearrange("p (a h d) -> p a h d", h=2, d=HD1)
                act.activation(v_pad[u][0:CTX, 4 * k:4 * k + 4, 0:4:3, :], src, ACT.Copy).then_inc(v_done, 1)

            def q_high(b, k):
                wait(act, pe_q, 4, b, k + 1)
                wait(act, pe_s, NG, b, 2 * k - 2)
                act.activation(q_hi[k % 2][:, :, :].rearrange("p a n -> p (a n)"), turn_ps[BANK[f"q_{k}"]][:, :],
                               ACT.Copy).then_inc(q_hi_done, 1)

            def exponentials(b, g):
                wait(act, max_done, NG, b, g + 1)
                wait(act, pe_pT, NG, b, g - 3)
                for h in range(HG):
                    last = act.activation(probs[g % 4][:, h, :], score_ps[g % 2][:, h * CTX:(h + 1) * CTX], ACT.Exp,
                                          bias=neg_max[:, g % 4, h:h + 1], accum_out=sums[:, g % 4, h:h + 1])
                last.then_inc(exp_done, 1)

            def pT_copy(b, g):
                hg, t = g // 2, g % 2
                wait(act, pe_pT, NG, b, g + 1)
                wait(act, pe_c, NHG, b, hg - 1)
                act.activation(pT[hg % 2][:, :, t * P:(t + 1) * P],
                               pT_ps[0:CTX, :].rearrange("p (h n) -> p h n", h=HG), ACT.Copy).then_inc(pT_done, 1)

            def c_high(b, hg):
                wait(act, pe_c, NHG, b, hg + 1)
                wait(act, pe_w, 2, b, 0)
                act.activation(c_hi[:, 2 * hg:2 * hg + 2, :].rearrange("p a n -> p (a n)"), c_ps[:, :],
                               ACT.Copy).then_inc(c_hi_done, 1)

            act.wait_ge(gamma_scaled, 1)
            act.wait_ge(stage_in[1], 64)
            small = ((w0q_hi[:, :, :], 0), (w0kv_hi[:, :, 0, :], 1), (w0kv_hi[:, :, 1, :], 1), (w0o_hi[:, :, :], None))
            for n, (dst, g) in enumerate(small):
                for ch in range(DC):
                    scale = 1.0 if g is None else gamma[:, g, ch:ch + 1]
                    last = act.activation(dst[:, ch], quarter[n][:, ch, :], ACT.Copy, scale=scale)
                last.then_inc(staged_hi, 1)
            act.wait_ge(const_done, 1)
            act.wait_ge(v_zeroed, 1)
            squares(0, 0)
            act.wait_ge(stage_in[0], 16)
            for ch in range(DC):
                last = act.activation(w1q_hi[:, ch, :], big[:, ch, :], ACT.Copy, scale=gamma[:, 2, ch:ch + 1])
            last.then_inc(staged_hi, 1)
            act.wait_ge(stage_in[1], 80)
            act.activation(w1v_hi[:, :, :].rearrange("p c n -> p (c n)"), stages[1], ACT.Copy).then_inc(staged_hi, 1)
            act.wait_ge(stage_in[0], 32)
            act.activation(w1o_hi[:, :, :].rearrange("p c n -> p (c n)"), stages[0], ACT.Copy).then_inc(staged_hi, 1)
            act.wait_ge(v_zeroed, 2)

            def slot(s, u, kind):
                front, back, more = kind < NB, kind >= 1, kind < NB - 1
                b = s - 1
                if front:
                    layer0_q(s, u)
                if back:
                    exponentials(b, 0)
                    q_high(b, 1)
                    exponentials(b, 1)
                if front:
                    kv_high(s, u)
                if back:
                    pT_copy(b, 0)
                if more:
                    squares(s + 1, 1 - u)
                if back:
                    exponentials(b, 2)
                if front:
                    v_copy(s, u, 0)
                if back:
                    q_high(b, 2)
                    pT_copy(b, 1)
                    exponentials(b, 3)
                    c_high(b, 0)
                    pT_copy(b, 2)
                    exponentials(b, 4)
                    pT_copy(b, 3)
                    q_high(b, 3)
                    exponentials(b, 5)
                    c_high(b, 1)
                    pT_copy(b, 4)
                    exponentials(b, 6)
                    pT_copy(b, 5)
                if front:
                    v_copy(s, u, 1)
                if front:
                    out_high(s)
                if back:
                    exponentials(b, 7)
                    c_high(b, 2)
                if front:
                    squares1(s, u)
                if back:
                    pT_copy(b, 6)
                if front:
                    normed1(s, u)
                    k_high(s, u, 0)
                if back:
                    pT_copy(b, 7)
                if front:
                    x1T_high(s)
                if back:
                    c_high(b, 3)
                if front:
                    k_high(s, u, 1)
                    q_high(s, 0)

            slots(act, slot)

        @block.vector
        def _(dve):
            def ctxT_high(c, u):
                wait_inputs(dve, c, u)
                wait(dve, pe_v, 2, c, 0)
                dve.tensor_copy(cT_hi[:, :, :], ctxT_in[u][:, :, :]).then_inc(cT_hi_done, 1)

            def xT_high(c, u):
                wait_inputs(dve, c, u)
                wait(dve, pe_q0, 1, c, 0)
                dve.tensor_copy(xT_hi[:, :, :], xT_in[u][:, :, :]).then_inc(xT_hi_done, 1)

            def kv_low(c, u):
                wait(dve, kv_hi_done, 1, c, 1)
                dve.scalar_tensor_tensor(out=kv_lo[:, :, :].rearrange("p a n -> p (a n)"), in0=turn_ps[BANK["kv0"]][0:CTX, :],
                                         scalar=rs[u][0:CTX, 2:3],
                                         in1=kv_hi[:, :, :].rearrange("p a n -> p (a n)").bitcast(F32),
                                         op0=ALU.mult, op1=ALU.subtract).then_inc(kv_done, 1)

            def low(dst, hi, src, hi_done, per, batch, n, done):
                wait(dve, hi_done, per, batch, n)
                dve.tensor_tensor(dst, src, hi.bitcast(F32), ALU.subtract).then_inc(done, 1)

            def scores0(c, t):
                if t == 0:
                    wait(dve, o0_done, 2, c, 0)
                else:
                    wait(dve, score0_done, 2, c, 1)
                wait(dve, pe_kg, 2, c, t + 1)
                wait(dve, q0_done, 1, c, 1)
                dve.tensor_tensor(prod[:, :].rearrange("p (j d) -> p j d", j=NEIGH),
                                  g_ps[:, 0:NEIGH * D].rearrange("p (j d) -> p j d", j=NEIGH),
                                  q0[:, t, :].unsqueeze(1).broadcast_to([P, NEIGH, D]), ALU.mult).then_inc(kprod_done, 1)
                wait(dve, kprod_done, 2, c, t + 1)
                dve.tensor_reduce(s0[:, t, :, :].rearrange("p j h -> p (j h)"),
                                  prod[:, :].rearrange("p (a e) -> p a e", e=HD0), X_AXIS, ALU.add).then_inc(score0_done, 1)

            def weights0(c):
                wait(dve, score0_done, 2, c, 2)
                flat = lambda a: a[:, :, :, :].rearrange("p t j h -> p (t j h)")
                dve.scalar_tensor_tensor(out=flat(w0), in0=flat(s0), scalar=0.0, in1=flat(s0),
                                         op0=ALU.max, op1=ALU.mult).then_inc(weight_steps, 1)
                wait(dve, weight_steps, 4, c, 1)
                dve.tensor_reduce(den[:, :, :], w0[:, :, :, :].rearrange("p t j h -> p t h j"), X_AXIS,
                                  ALU.add).then_inc(weight_steps, 1)
                wait(dve, weight_steps, 4, c, 2)
                dve.tensor_scalar(den_c[:, :, :], den[:, :, :], EPS_DEN, None, ALU.max).then_inc(weight_steps, 1)
                wait(dve, weight_steps, 4, c, 3)
                dve.reciprocal(rden[:, :, :], den_c[:, :, :]).then_inc(weight_steps, 1)
                wait(dve, weight_steps, 4, c, 4)
                dve.tensor_tensor(wn[:, :, :, :], w0[:, :, :, :],
                                  rden[:, :, :].unsqueeze(2).broadcast_to([P, TT, NEIGH, H0]), ALU.mult).then_inc(weights_done, 1)

            def value_products0(c, t):
                wait(dve, pe_vg, 2, c, t + 1)
                wait(dve, weights_done, 1, c, 1)
                if t == 1:
                    wait(dve, o0_done, 2, c, 1)
                dve.tensor_tensor(prod[:, :].rearrange("p (a e) -> p a e", e=HD0),
                                  g_ps[:, 0:NEIGH * D].rearrange("p (a e) -> p a e", e=HD0),
                                  wn[:, t, :, :].rearrange("p j h -> p (j h)").unsqueeze(2).broadcast_to([P, NEIGH * H0, HD0]),
                                  ALU.mult).then_inc(vprod_done, 1)

            def value_sums0(c, t):
                wait(dve, vprod_done, 2, c, t + 1)
                if t == 1:
                    wait(dve, o0_done, 2, c, 1)
                dve.tensor_tensor(o01[:, :], prod[:, 0:D], prod[:, D:2 * D], ALU.add).then_inc(pair_sum_done, 1)
                wait(dve, pair_sum_done, 2, c, t + 1)
                if t == 0:
                    wait(dve, pe_xT, 1, c, 0)
                dve.tensor_tensor(o0[:, t, :], o01[:, :], prod[:, 2 * D:3 * D], ALU.add).then_inc(o0_done, 1)

            def residual0(c, u):
                wait(dve, pe_oW, 1, c, 1)
                wait_inputs(dve, c, u)
                dve.tensor_tensor(x1[u][:, :, :].rearrange("p t d -> p (t d)"), turn_ps[BANK["oW"]][:, :],
                                  x_in[u][:, :, :].rearrange("p t d -> p (t d)"), ALU.add).then_inc(x1_done, 1)

            def k_low(c, u, k):
                wait(dve, k_hi_done, 2, c, k + 1)
                src = g_ps[:, k * 512:k * 512 + 4 * CTX].rearrange("p (c n) -> p c n", c=4)
                for h in range(2):
                    rows = slice(h * HD1, (h + 1) * HD1)
                    at = (rows, slice(4 * k, 4 * k + 4), slice(h * CTX, (h + 1) * CTX))
                    last = dve.tensor_tensor(k_lo[u][at], src[rows], k_hi[u][at].bitcast(F32), ALU.subtract)
                last.then_inc(k_done, 1)

            def q_low(b, k):
                low(q_lo[k % 2][:, :, :].rearrange("p a n -> p (a n)"), q_hi[k % 2][:, :, :].rearrange("p a n -> p (a n)"),
                    turn_ps[BANK[f"q_{k}"]][:, :], q_hi_done, 4, b, k + 1, q_done)

            def c_low(b, hg):
                low(c_lo[:, 2 * hg:2 * hg + 2, :].rearrange("p a n -> p (a n)"),
                    c_hi[:, 2 * hg:2 * hg + 2, :].rearrange("p a n -> p (a n)"), c_ps[:, :], c_hi_done, NHG, b, hg + 1, c_done)

            def maxima(b, g):
                wait(dve, pe_s, NG, b, g + 1)
                view = score_ps[g % 2][:, 0:GC].rearrange("p (h n) -> p h n", h=HG)
                dve.tensor_reduce(neg_max[:, g % 4, :], view, X_AXIS, ALU.max, negate=True).then_inc(max_done, 1)

            def recip(b, g):
                wait(dve, exp_done, NG, b, g + 1)
                dve.reciprocal(rsum[:, g % 4, :], sums[:, g % 4, :]).then_inc(rsum_done, 1)

            def result(b, u, t):
                wait(dve, pe_w, 2, b, t + 1)
                if t == 0:
                    wait(dve, y_out, 16, b, 0)
                dve.tensor_tensor(y[:, t, :], turn_ps[BANK[f"w{t}"]][:, 0:D], x1[u][:, t, :], ALU.add).then_inc(y_done, 1)

            dve.wait_ge(gamma_in, 16)
            dve.tensor_scalar(gamma[:, 0, :], gamma[:, 0, :], HD0 ** -0.5, None, ALU.mult).then_inc(gamma_scaled, 1)
            for u in range(2):
                last = dve.memset(ms[u][:, :], 1.0)
            last.then_inc(v_zeroed, 1)
            dve.wait_ge(const_steps, 5)
            dve.tensor_copy(pos[:, :], pos_i[:, :]).then_inc(pos_done, 1)
            for u in range(2):
                dve.memset(k_hi[u][:, :, :].bitcast(F32), 0.0)
                last = dve.memset(k_lo[u][:, :, :].bitcast(F32), 0.0)
            last.then_inc(k_zeroed, 1)
            xT_high(0, 0)
            ctxT_high(0, 0)
            dve.wait_ge(gamma_scaled, 1)
            small = ((w0q_hi[:, :, :], w0q_lo[:, :, :], 0), (w0kv_hi[:, :, 0, :], w0kv_lo[:, :, 0, :], 1),
                     (w0kv_hi[:, :, 1, :], w0kv_lo[:, :, 1, :], 1), (w0o_hi[:, :, :], w0o_lo[:, :, :], None))
            for n, (hi, lo, g) in enumerate(small):
                dve.wait_ge(staged_hi, n + 1)
                for ch in range(DC):
                    scale = 1.0 if g is None else gamma[:, g, ch:ch + 1]
                    last = dve.scalar_tensor_tensor(out=lo[:, ch], in0=quarter[n][:, ch, :], scalar=scale,
                                                    in1=hi[:, ch].bitcast(F32), op0=ALU.mult, op1=ALU.subtract)
                last.then_inc(stage_split, 1)
            dve.wait_ge(staged_hi, 5)
            for ch in range(DC):
                last = dve.scalar_tensor_tensor(out=w1q_lo[:, ch, :], in0=big[:, ch, :], scalar=gamma[:, 2, ch:ch + 1],
                                                in1=w1q_hi[:, ch, :].bitcast(F32), op0=ALU.mult, op1=ALU.subtract)
            last.then_inc(stage_split, 1)
            for n, (hi, lo, stage) in enumerate(((w1v_hi, w1v_lo, stages[1]), (w1o_hi, w1o_lo, stages[0]))):
                dve.wait_ge(staged_hi, 6 + n)
                dve.tensor_tensor(lo[:, :, :].rearrange("p c n -> p (c n)"), stage,
                                  hi[:, :, :].rearrange("p c n -> p (c n)").bitcast(F32), ALU.subtract).then_inc(stage_split, 1)
            dve.wait_ge(stage_split, 7)
            for u in range(2):
                last = dve.memset(v_pad[u][:, :, :, :], 0.0)
            last.then_inc(v_zeroed, 1)

            def slot(s, u, kind):
                front, back, older, more = kind < NB, kind >= 1, kind >= 2, kind < NB - 1
                b = s - 1
                if back:
                    maxima(b, 0)
                    recip(b, 0)
                    q_low(b, 1)
                    maxima(b, 1)
                    recip(b, 1)
                if older:
                    result(s - 2, u, 1)
                if front:
                    kv_low(s, u)
                if back:
                    maxima(b, 2)
                    recip(b, 2)
                if front:
                    scores0(s, 0)
                if back:
                    q_low(b, 2)
                    maxima(b, 3)
                if front:
                    scores0(s, 1)
                if back:
                    recip(b, 3)
                    maxima(b, 4)
                    c_low(b, 0)
                if front:
                    weights0(s)
                if back:
                    recip(b, 4)
                if front:
                    value_products0(s, 0)
                if back:
                    q_low(b, 3)
                    maxima(b, 5)
                if front:
                    value_sums0(s, 0)
                    value_products0(s, 1)
                if back:
                    recip(b, 5)
                    maxima(b, 6)
                if front:
                    value_sums0(s, 1)
                if back:
                    c_low(b, 1)
                    recip(b, 6)
                    maxima(b, 7)
                if front:
                    low(oT_lo[:, :, :].rearrange("p a n -> p (a n)"), oT_hi[:, :, :].rearrange("p a n -> p (a n)"),
                        turn_ps[BANK["oT"]][:, :], oT_hi_done, 1, s, 1, oT_done)
                if back:
                    c_low(b, 2)
                    recip(b, 7)
                if front:
                    residual0(s, u)
                if more:
                    xT_high(s + 1, 1 - u)
                    ctxT_high(s + 1, 1 - u)
                if front:
                    k_low(s, u, 0)
                    low(x1T_lo[:, :, :].rearrange("p a n -> p (a n)"), x1T_hi[:, :, :].rearrange("p a n -> p (a n)"),
                        turn_ps[BANK["xT"]][:, :], x1T_hi_done, 1, s, 1, x1T_done)
                if back:
                    c_low(b, 3)
                if front:
                    q_low(s, 0)
                    k_low(s, u, 1)
                if back:
                    result(b, 1 - u, 0)

            slots(dve, slot)
            result(NB - 1, 1, 1)

        @block.tensor
        def _(pe):
            def take_bank(name, s, kind):
                before = turn_before(name, kind)
                if before:
                    name_before, rel = before
                    done, per, n = EMPTIED[name_before]
                    wait(pe, done, per, s + rel, n)
                return turn_ps[BANK[name]]

            def split_product(dst, pairs):
                todo = [(a, b) for (a_hi, a_lo), (b_hi, b_lo) in pairs
                        for a, b in ((a_hi, b_hi), (a_hi, b_lo), (a_lo, b_hi))]
                for n, (a, b) in enumerate(todo):
                    last = pe.matmul(dst, a, b, start=n == 0, stop=n == len(todo) - 1)
                return last

            def layer0_q(c):
                wait(pe, k_done, 2, c, -1)
                wait(pe, xT_done, 1, c, 1)
                for t in range(TT):
                    rows = slice(t * P, (t + 1) * P)
                    last = split_product(g_ps[:, t * D:(t + 1) * D],
                                         [((xT_hi[:, ch, rows], xT_lo[:, ch, rows]), (w0q_hi[:, ch, :], w0q_lo[:, ch, :]))
                                          for ch in range(DC)])
                last.then_inc(pe_q0, 1)

            def layer0_kv(c, kind):
                bank = take_bank("kv0", c, kind)
                wait(pe, cT_done, 1, c, 1)
                split_product(bank[0:CTX, :],
                              [((cT_hi[:, ch, :], cT_lo[:, ch, :]),
                                (w0kv_hi[:, ch, :, :].rearrange("p a n -> p (a n)"), w0kv_lo[:, ch, :, :].rearrange("p a n -> p (a n)")))
                               for ch in range(DC)]).then_inc(pe_kv0, 1)

            def gather(c, t, part, done):
                for j in range(NEIGH):
                    for n, kv in enumerate((kv_hi, kv_lo)):
                        last = pe.matmul(g_ps[:, j * D:(j + 1) * D], onehot[:, j, t * P:(t + 1) * P], kv[:, part, :],
                                         start=n == 0, stop=n == 1)
                last.then_inc(done, 1)

            def gather_k(c, t):
                if t == 0:
                    wait(pe, kv_done, 1, c, 1)
                    wait(pe, onehot_done, 1, c, 1)
                    wait(pe, q0_done, 1, c, 1)
                    wait(pe, k_done, 2, c, 0)
                else:
                    wait(pe, kprod_done, 2, c, 1)
                gather(c, t, 0, pe_kg)

            def gather_v(c, t):
                if t == 0:
                    wait(pe, kprod_done, 2, c, 2)
                else:
                    wait(pe, vprod_done, 2, c, 1)
                gather(c, t, 1, pe_vg)

            def transposes(bank, src, done):
                for ch in range(DC):
                    for t in range(TT):
                        last = pe.transpose(bank[:, ch * T + t * P:ch * T + (t + 1) * P], src[:, t, ch * P:(ch + 1) * P], ident[:, :])
                last.then_inc(done, 1)

            def out_transposed(c, kind):
                bank = take_bank("oT", c, kind)
                wait(pe, o0_done, 2, c, 2)
                transposes(bank, o0, pe_oT)

            def out_product(c, kind):
                bank = take_bank("oW", c, kind)
                wait(pe, oT_done, 1, c, 1)
                for t in range(TT):
                    rows = slice(t * P, (t + 1) * P)
                    last = split_product(bank[:, t * D:(t + 1) * D],
                                         [((oT_hi[:, ch, rows], oT_lo[:, ch, rows]), (w0o_hi[:, ch, :], w0o_lo[:, ch, :]))
                                          for ch in range(DC)])
                last.then_inc(pe_oW, 1)

            def x1_transposed(c, kind):
                bank = take_bank("xT", c, kind)
                wait(pe, x1n_done, 1, c, 1)
                transposes(bank, x1n, pe_xT)

            def keys(c, u, k):
                wait(pe, vprod_done, 2, c, 2)
                wait_inputs(pe, c, u)
                bank = g_ps[:, k * 512:(k + 1) * 512]
                for n in range(4):
                    cols = slice((4 * k + n) * P, (4 * k + n + 1) * P)
                    for ch in range(DC):
                        last = pe.matmul(bank[:, n * CTX:(n + 1) * CTX], w1k_sb[:, ch, cols], ctxT_in[u][:, ch, :],
                                         start=ch == 0, stop=ch == DC - 1)
                last.then_inc(pe_k, 1)

            def values(c, k, kind):
                bank = take_bank(f"v_{k}", c, kind)
                wait(pe, cT_done, 1, c, 1)
                cols = slice(k * 512, (k + 1) * 512)
                split_product(bank[0:CTX, :], [((cT_hi[:, ch, :], cT_lo[:, ch, :]), (w1v_hi[:, ch, cols], w1v_lo[:, ch, cols]))
                                               for ch in range(DC)]).then_inc(pe_v, 1)

            def queries(b, s, k, kind):
                bank = take_bank(f"q_{k}", s, kind)
                wait(pe, x1T_done, 1, b, 1)
                for n in range(2):
                    cols = slice((2 * k + n) * P, (2 * k + n + 1) * P)
                    last = split_product(bank[:, n * T:(n + 1) * T],
                                         [((w1q_hi[:, ch, cols], w1q_lo[:, ch, cols]), (x1T_hi[:, ch, :], x1T_lo[:, ch, :]))
                                          for ch in range(DC)])
                last.then_inc(pe_q, 1)

            def scores(b, u, g):
                hg, t = g // 2, g % 2
                if t == 0:
                    wait(pe, q_done, 4, b, hg + 1)
                    if hg % 2 == 0:
                        wait(pe, k_done, 2, b, hg // 2 + 1)
                before, batch = (g - 2, b) if g >= 2 else (g + 6, b - 1)
                wait(pe, exp_done, NG, batch, before + 1)
                for n in range(2):
                    pair, rows = 2 * hg + n, slice(t * P, (t + 1) * P)
                    last = split_product(score_ps[g % 2][:, n * 2 * CTX:(n + 1) * 2 * CTX],
                                         [((q_hi[hg % 2][:, n, rows], q_lo[hg % 2][:, n, rows]), (k_hi[u][:, pair, :], k_lo[u][:, pair, :]))])
                last.then_inc(pe_s, 1)

            def probs_transposed(b, g):
                wait(pe, norm_done, NG, b, g + 1)
                wait(pe, pT_done, NG, b, g)
                for h in range(HG):
                    last = pe.transpose(pT_ps[0:CTX, h * P:(h + 1) * P], probs[g % 4][:, h, :], ident[:, :])
                last.then_inc(pe_pT, 1)

            def mix(b, u, hg):
                wait(pe, pT_done, NG, b, 2 * hg + 2)
                if hg % 2 == 0:
                    wait(pe, v_done, 2, b, hg // 2 + 1)
                wait(pe, c_done, NHG, b, hg)
                for n in range(2):
                    for h in range(2):
                        last = pe.matmul(c_ps[:, n * T:(n + 1) * T],
                                         v_pad[u][0:CTX, 2 * hg + n, 2 * h:2 * h + 2, :].rearrange("p a d -> p (a d)"),
                                         pT[hg % 2][:, 2 * n + h, :], start=h == 0, stop=h == 1)
                last.then_inc(pe_c, 1)

            def output(bank, b, t, first, end):
                wait(pe, c_done, NHG, b, end // 2)
                rows = slice(t * P, (t + 1) * P)
                todo = [(a, w) for ch in range(first, end)
                        for a, w in ((c_hi[:, ch, rows], w1o_hi[:, ch, :]), (c_hi[:, ch, rows], w1o_lo[:, ch, :]),
                                     (c_lo[:, ch, rows], w1o_hi[:, ch, :]))]
                for n, (a, w) in enumerate(todo):
                    last = pe.matmul(bank[:, 0:D], a, w, start=first == 0 and n == 0,
                                     stop=end == EC and n == len(todo) - 1)
                if end == EC:
                    last.then_inc(pe_w, 1)

            pe.wait_ge(const_done, 1)
            pe.wait_ge(k_zeroed, 1)
            pe.wait_ge(v_zeroed, 1)
            pe.wait_ge(stage_split, 4)

            def slot(s, u, kind):
                front, back, older = kind < NB, kind >= 1, kind >= 2
                b = s - 1
                if front:
                    layer0_q(s)
                if back:
                    scores(b, 1 - u, 0)
                    queries(b, s, 1, kind)
                    scores(b, 1 - u, 1)
                if older:
                    output(take_bank("w1", s, kind), s - 2, 1, 0, EC)
                if front:
                    layer0_kv(s, kind)
                if back:
                    probs_transposed(b, 0)
                    scores(b, 1 - u, 2)
                if front:
                    if kind == 0:
                        pe.wait_ge(stage_split, 6)
                    values(s, 0, kind)
                    gather_k(s, 0)
                if back:
                    queries(b, s, 2, kind)
                    probs_transposed(b, 1)
                    scores(b, 1 - u, 3)
                if front:
                    gather_k(s, 1)
                if back:
                    mix(b, 1 - u, 0)
                    probs_transposed(b, 2)
                    scores(b, 1 - u, 4)
                    queries(b, s, 3, kind)
                if front:
                    gather_v(s, 0)
                if back:
                    probs_transposed(b, 3)
                    scores(b, 1 - u, 5)
                    mix(b, 1 - u, 1)
                if front:
                    gather_v(s, 1)
                if back:
                    probs_transposed(b, 4)
                    scores(b, 1 - u, 6)
                if front:
                    values(s, 1, kind)
                if back:
                    probs_transposed(b, 5)
                    scores(b, 1 - u, 7)
                if front:
                    out_transposed(s, kind)
                if back:
                    mix(b, 1 - u, 2)
                if front:
                    out_product(s, kind)
                if back:
                    probs_transposed(b, 6)
                if front:
                    if kind == 0:
                        pe.wait_ge(w1k_in, 16)
                    keys(s, u, 0)
                if back:
                    half_done = take_bank("w0", s, kind)
                    output(half_done, b, 0, 0, 4)
                    probs_transposed(b, 7)
                    output(half_done, b, 0, 4, 6)
                if front:
                    x1_transposed(s, kind)
                if back:
                    mix(b, 1 - u, 3)
                if front:
                    keys(s, u, 1)
                    queries(s, s, 0, kind)
                if back:
                    output(half_done, b, 0, 6, EC)

            slots(pe, slot)
            output(take_bank("w1", NB + 1, NB + 1), NB - 1, 1, 0, EC)


def kernel(x, ctx_1024, itok_BxS_0_255, L0_xattn_gamma_q, L0_xattn_gamma_kv, L0_xattn_Wq, L0_xattn_Wk, L0_xattn_Wv,
           L0_xattn_Wo, L1_xattn_wq, L1_xattn_wk, L1_xattn_wv, L1_xattn_wo, L1_xattn_norm_w):
    import numpy as np
    import concourse.bacc as bacc
    from concourse.bass_utils import run_bass_kernel_spmd

    turned = lambda a, *axes: np.ascontiguousarray(np.transpose(np.asarray(a), axes))
    plain = lambda a: np.ascontiguousarray(np.asarray(a))
    arrays = {
        "x": plain(x), "xT": turned(x, 0, 2, 1), "ctx": plain(ctx_1024), "ctxT": turned(ctx_1024, 0, 2, 1),
        "idx": plain(itok_BxS_0_255), 
        "gammas": turned(np.stack([plain(g).reshape(DC, P) for g in
                                   (L0_xattn_gamma_q, L0_xattn_gamma_kv, L1_xattn_norm_w)]), 2, 0, 1),
        "w0qT": turned(L0_xattn_Wq, 1, 0), "w0kT": turned(L0_xattn_Wk, 1, 0), "w0vT": turned(L0_xattn_Wv, 1, 0),
        "w0oT": turned(L0_xattn_Wo, 1, 0), "w1q": plain(L1_xattn_wq), "w1k": plain(L1_xattn_wk),
        "w1v": plain(L1_xattn_wv), "w1o": plain(L1_xattn_wo),
    }
    nc = bacc.Bacc("TRN2", target_bir_lowering=False, num_devices=1)
    aps = {n: nc.dram_tensor(f"in_{n}", a.shape, mybir.dt.from_np(a.dtype), kind="ExternalInput").ap()
           for n, a in arrays.items()}
    out = nc.dram_tensor("out", (NB, T, D), F32, kind="ExternalOutput").ap()
    build(nc, **aps, out=out)
    r = run_bass_kernel_spmd(nc, [{f"in_{n}": a for n, a in arrays.items()}], core_ids=[0])
    return r.results[0]["out"]
```

```python
from contextlib import ExitStack

import concourse.bass as bass
from concourse import mybir
from concourse.alu_op_type import AluOpType as ALU

F32 = mybir.dt.float32
F32R = mybir.dt.float32r
I32 = mybir.dt.int32
ACT = mybir.ActivationFunctionType
X_AXIS = mybir.AxisListType.X

P = 128
NB, T, D = 32, 256, 256
CTX = 120
H0, HD0 = 16, 16
H1, HD1 = 16, 64
E1 = H1 * HD1
TT = T // P
DC = D // P
EC = E1 // P
NEIGH = 3
HG = 4
NHG = H1 // HG
NG = NHG * TT
GC = HG * CTX
LOADS = 5
ROOT = D ** -0.5
EPS0, EPS1, EPS_DEN = 1.1920929e-07, 1e-06, 1e-06

TURNS = [("q_1", -1, 0), ("w1", -2, 1), ("kv0", 0, 0), ("v_0", 0, 1), ("q_2", -1, 0), ("q_3", -1, 0),
         ("v_1", 0, 0), ("oT", 0, 1), ("oW", 0, 1), ("w0", -1, 1), ("xT", 0, 0), ("q_0", 0, 0)]
BANK = {name: bank for name, _, bank in TURNS}


def turn_before(name, s):
    at = [n for n, _, _ in TURNS].index(name)
    back = [(n, rel) for n, rel, _ in reversed(TURNS[:at])] + [(n, rel - 1) for n, rel, _ in reversed(TURNS)]
    for n, rel in back:
        if BANK[n] == BANK[name] and 0 <= s + rel < NB:
            return n, rel
    return None


def build(nc, x, xT, ctx, ctxT, idx, gammas, w0qT, w0kT, w0vT, w0oT, w1q, w1k, w1v, w1o, out):
    st = ExitStack()
    with st:
        def sb(name, shape, dt=F32):
            return st.enter_context(nc.sbuf_tensor(name, shape, dt))

        def ps(name, shape):
            return st.enter_context(nc.psum_tensor(name, shape, F32))

        def sem(name):
            return st.enter_context(nc.semaphore(name))

        w0q_hi, w0q_lo = sb("w0q_hi", [P, DC, D], F32R), sb("w0q_lo", [P, DC, D], F32R)
        w0kv_hi, w0kv_lo = sb("w0kv_hi", [P, DC, 2, D], F32R), sb("w0kv_lo", [P, DC, 2, D], F32R)
        w0o_hi, w0o_lo = sb("w0o_hi", [P, DC, D], F32R), sb("w0o_lo", [P, DC, D], F32R)
        w1q_hi, w1q_lo = sb("w1q_hi", [P, DC, E1], F32R), sb("w1q_lo", [P, DC, E1], F32R)
        w1v_hi, w1v_lo = sb("w1v_hi", [P, DC, E1], F32R), sb("w1v_lo", [P, DC, E1], F32R)
        w1o_hi, w1o_lo = sb("w1o_hi", [P, EC, D], F32R), sb("w1o_lo", [P, EC, D], F32R)
        w1k_sb = sb("w1k_sb", [P, DC, E1])
        w1q_raw, w1o_raw = sb("w1q_raw", [P, DC, E1]), sb("w1o_raw", [P, EC, D])
        gamma = sb("gamma", [P, 3, DC])
        ident = sb("ident", [P, P])
        pos_i = sb("pos_i", [P, NEIGH], I32)
        pos = sb("pos", [P, NEIGH])
        small_consts = sb("small_consts", [P, 8])
        eps0, eps1 = small_consts[:, 0:3], small_consts[:, 3:5]
        half = small_consts[:, 5:8]
        x_in = [sb(f"x_in{u}", [P, TT, D]) for u in range(2)]
        xT_in = [sb(f"xT_in{u}", [P, DC, T]) for u in range(2)]
        ctx_in = [sb(f"ctx_in{u}", [CTX, D]) for u in range(2)]
        ctxT_in = [sb(f"ctxT_in{u}", [P, DC, CTX]) for u in range(2)]
        idx_in = [sb(f"idx_in{u}", [CTX, T], I32) for u in range(2)]
        junk = sb("junk", [P, 5, D], mybir.dt.bfloat16)
        ms = [sb(f"ms_{u}", [P, 3]) for u in range(2)]
        ms_eps = sb("ms_eps", [P, 3])
        rs = [sb(f"rs_{u}", [P, 3]) for u in range(2)]
        xT_hi, xT_lo = sb("xT_hi", [P, DC, T], F32R), sb("xT_lo", [P, DC, T], F32R)
        cT_hi, cT_lo = sb("cT_hi", [P, DC, CTX], F32R), sb("cT_lo", [P, DC, CTX], F32R)
        onehot = sb("onehot", [CTX, NEIGH, T], F32R)
        q0 = sb("q0", [P, TT, D])
        kv_hi, kv_lo = sb("kv_hi", [CTX, 2, D], F32R), sb("kv_lo", [CTX, 2, D], F32R)
        prod = [sb(f"prod{t}", [P, NEIGH * D]) for t in range(TT)]
        s0 = sb("s0", [P, TT, NEIGH, H0])
        w0 = sb("w0", [P, TT, NEIGH, H0])
        den = sb("den", [P, TT, H0])
        den_c = sb("den_c", [P, TT, H0])
        rden = sb("rden", [P, TT, H0])
        wn = sb("wn", [P, TT, NEIGH, H0])
        o0 = sb("o0", [P, TT, D])
        x1 = [sb(f"x1_{u}", [P, TT, D]) for u in range(2)]
        ms1, ms1_eps, rs1 = sb("ms1", [P, TT]), sb("ms1_eps", [P, TT]), sb("rs1", [P, TT])
        x1n = o0
        x1T_hi, x1T_lo = sb("x1T_hi", [P, DC, T], F32R), sb("x1T_lo", [P, DC, T], F32R)
        oT_hi, oT_lo = x1T_hi, x1T_lo
        q_hi = [sb(f"q_hi{n}", [P, 2, T], F32R) for n in range(2)]
        q_lo = [sb(f"q_lo{n}", [P, 2, T], F32R) for n in range(2)]
        k_hi, k_lo = sb("k_hi", [P, EC, 2 * CTX], F32R), sb("k_lo", [P, EC, 2 * CTX], F32R)
        v_sb = sb("v_sb", [P, 2, E1])
        neg_max = sb("neg_max", [P, 4, HG])
        sums = sb("sums", [P, 4, HG])
        rsum = sb("rsum", [P, 4, HG])
        probs = [sb(f"probs{n}", [P, HG, CTX]) for n in range(4)]
        pT_sb = sb("pT_sb", [P, 2, HG, T])
        c_hi, c_lo = sb("c_hi", [P, EC, T], F32R), sb("c_lo", [P, EC, T], F32R)
        y = sb("y", [P, TT, D])

        score_ps = [ps(f"score_ps{n}", [P, 512]) for n in range(2)]
        pT_ps = ps("pT_ps", [P, 512])
        c_ps = ps("c_ps", [P, 512])
        g_ps = ps("g_ps", [P, 1024])
        turn_ps = [ps(f"turn_ps{n}", [P, 512]) for n in range(2)]

        inputs_in = [sem(f"inputs_in{u}") for u in range(2)]
        y_out = sem("y_out")
        gamma_in, w1k_in = sem("gamma_in"), sem("w1k_in")
        small_in = [sem(f"{n}_in") for n in ("w0q", "w0k", "w0v", "w0o")]
        w1v_in, w1q_in, w1o_in = sem("w1v_in"), sem("w1q_in"), sem("w1o_in")
        small_hi, small_split = sem("small_hi"), sem("small_split")
        w1v_hi_done, w1v_done = sem("w1v_hi_done"), sem("w1v_done")
        w1q_hi_done, w1q_done = sem("w1q_hi_done"), sem("w1q_done")
        w1o_hi_done, w1o_done = sem("w1o_hi_done"), sem("w1o_done")
        gamma_scaled = sem("gamma_scaled")
        ms_set, k_zeroed = sem("ms_set"), sem("k_zeroed")
        const_steps, const_done, pos_done = sem("const_steps"), sem("const_done"), sem("pos_done")
        pe_q0, pe_kv0, pe_kg, pe_vg = sem("pe_q0"), sem("pe_kv0"), sem("pe_kg"), sem("pe_vg")
        pe_oT, pe_oW, pe_xT = sem("pe_oT"), sem("pe_oW"), sem("pe_xT")
        pe_k, pe_v, pe_q, pe_s = sem("pe_k"), sem("pe_v"), sem("pe_q"), sem("pe_s")
        pe_pT, pe_c, pe_w = sem("pe_pT"), sem("pe_c"), sem("pe_w")
        ms_done, q0_done, kv_hi_done, oT_hi_done = sem("ms_done"), sem("q0_done"), sem("kv_hi_done"), sem("oT_hi_done")
        ms1_done, x1n_done, x1T_hi_done = sem("ms1_done"), sem("x1n_done"), sem("x1T_hi_done")
        k_hi_done, v_done, q_hi_done = sem("k_hi_done"), sem("v_done"), sem("q_hi_done")
        exp_done, pT_done, c_hi_done = sem("exp_done"), sem("pT_done"), sem("c_hi_done")
        cT_hi_done, xT_hi_done, kv_done = sem("cT_hi_done"), sem("xT_hi_done"), sem("kv_done")
        kprod_done, score0_done, weight_steps, weights_done = sem("kprod_done"), sem("score0_done"), sem("weight_steps"), sem("weights_done")
        vprod_done, pair_sum_done, o0_done, oT_done = sem("vprod_done"), sem("pair_sum_done"), sem("o0_done"), sem("oT_done")
        x1_done, x1T_done, k_done, q_done = sem("x1_done"), sem("x1T_done"), sem("k_done"), sem("q_done")
        max_done, rsum_done = sem("max_done"), sem("rsum_done")
        c_done, y_done = sem("c_done"), sem("y_done")
        cT_done, xT_done, ms_eps_done, rs_done = sem("cT_done"), sem("xT_done"), sem("ms_eps_done"), sem("rs_done")
        onehot_done, ms1_eps_done, rs1_done, norm_done = sem("onehot_done"), sem("ms1_eps_done"), sem("rs1_done"), sem("norm_done")

        def wait(eng, s, per_batch, batch, n):
            value = batch * per_batch + n
            if not isinstance(value, int) or value > 0:
                eng.wait_ge(s, value)

        def wait_inputs(eng, batch, u):
            eng.wait_ge(inputs_in[u], (batch - u) * (LOADS * 8) + LOADS * 16)

        def slots(eng, slot):
            slot(0, 0, 0)
            slot(1, 1, 1)
            with eng.Fori(1, NB // 2 - 1) as pair:
                slot(pair * 2, 0, 2)
                slot(pair * 2 + 1, 1, 3)
            slot(NB - 2, 0, NB - 2)
            slot(NB - 1, 1, NB - 1)
            slot(NB, 0, NB)

        EMPTIED = {"kv0": (kv_done, 1, 1), "oT": (oT_done, 1, 1),
                   "oW": (x1_done, 1, 1), "xT": (x1T_done, 1, 1),
                   "w0": (y_done, 2, 1), "w1": (y_done, 2, 2),
                   "v_0": (v_done, 2, 1), "v_1": (v_done, 2, 2),
                   "q_0": (q_done, 4, 1), "q_1": (q_done, 4, 2), "q_2": (q_done, 4, 3), "q_3": (q_done, 4, 4)}

        small_stage = pT_sb[:, :, :, :].rearrange("p a (w b) c -> p (a w) (b c)", w=2)
        small_stage = [small_stage[:, n, :].rearrange("p (c n) -> p c n", c=DC) for n in range(4)]
        w1v_stage = v_sb[:, :, :]
        w1q_stage, w1o_stage = w1q_raw[:, :, :], w1o_raw[:, :, :]

        block = st.enter_context(nc.Block())

        @block.sync
        def _(sp):
            def load(batch, u):
                one = bass.ds(batch, 1)
                for dst, src in (
                    (xT_in[u][:, :, :], xT[one].rearrange("a (c p) t -> p (a c) t", p=P)),
                    (ctxT_in[u][:, :, :], ctxT[one].rearrange("a (c p) t -> p (a c) t", p=P)),
                    (x_in[u][:, :, :], x[one].rearrange("a (t p) d -> p (a t) d", p=P)),
                    (ctx_in[u][:, :], ctx[one].rearrange("a p d -> (a p) d")),
                    (idx_in[u][:, :], idx[one].to_broadcast([CTX, T])),
                ):
                    sp.dma_start(dst, src).then_inc(inputs_in[u], 16)

            def load_weight(dst, w, done):
                sp.dma_start(dst, w.rearrange("(c p) n -> p c n", p=P)).then_inc(done, 16)

            sp.dma_start(gamma[:, :, :], gammas).then_inc(gamma_in, 16)
            load_weight(small_stage[0], w0qT, small_in[0])
            load(0, 0)
            load_weight(small_stage[1], w0kT, small_in[1])
            load_weight(small_stage[2], w0vT, small_in[2])
            load_weight(w1v_stage, w1v, w1v_in)
            load_weight(small_stage[3], w0oT, small_in[3])
            load_weight(w1q_stage, w1q, w1q_in)
            load_weight(w1k_sb[:, :, :], w1k, w1k_in)
            load(1, 1)
            load_weight(w1o_stage, w1o, w1o_in)

            def store(batch):
                wait(sp, y_done, 2, batch, 2)
                sp.dma_start(out[bass.ds(batch, 1)].rearrange("a (t p) d -> p (a t) d", p=P),
                             y[:, :, :]).then_inc(y_out, 16)

            def slot(s, u, kind):
                if kind >= 2:
                    store(s - 2)
                if kind < NB - 2:
                    wait(sp, x1_done, 1, s, 1)
                    wait(sp, rs_done, 1, s, 1)
                    wait(sp, xT_done, 1, s, 1)
                    wait(sp, cT_done, 1, s, 1)
                    wait(sp, pe_k, 2, s, 2)
                    wait(sp, onehot_done, 1, s, 1)
                    load(s + 2, u)

            slots(sp, slot)
            store(NB - 1)
            sp.wait_ge(y_out, 16 * NB)

        @block.gpsimd
        def _(pool):
            pool.memset(ident[:, :], 0.0).then_inc(const_steps, 1)
            pool.iota(pos_i[:, :], [[-1, NEIGH]], base=1, channel_multiplier=1).then_inc(const_steps, 1)
            pool.memset(eps0[:, :], EPS0).then_inc(const_steps, 1)
            pool.memset(eps1[:, :], EPS1).then_inc(const_steps, 1)
            pool.memset(half[:, :], -0.5).then_inc(const_steps, 1)
            pool.wait_ge(const_steps, 5)
            pool.affine_select(out=ident[:, :], in_=ident[:, :], compare_op=ALU.not_equal, fill=1.0,
                               base=0, pattern=[[-1, P]], channel_multiplier=1).then_inc(const_done, 1)

            def split_ctxT(c, u):
                wait(pool, cT_hi_done, 1, c, 1)
                wait_inputs(pool, c, u)
                pool.tensor_tensor(cT_lo[:, :, :], ctxT_in[u][:, :, :], cT_hi[:, :, :].bitcast(F32),
                                   ALU.subtract).then_inc(cT_done, 1)

            def split_xT(c, u):
                wait(pool, xT_hi_done, 1, c, 1)
                wait_inputs(pool, c, u)
                pool.tensor_tensor(xT_lo[:, :, :], xT_in[u][:, :, :], xT_hi[:, :, :].bitcast(F32),
                                   ALU.subtract).then_inc(xT_done, 1)

            def root0(c, u, kind=None):
                wait(pool, ms_done, 1, c, 1)
                pool.tensor_tensor(ms_eps[:, :], ms[u][:, :], eps0[:, :], ALU.add).then_inc(ms_eps_done, 1)
                wait(pool, ms_eps_done, 1, c, 1)
                pool.tensor_tensor(rs[u][:, :], ms_eps[:, :], half[:, 0:3], ALU.pow).then_inc(rs_done, 1)
                if kind == 0:
                    w1o_low()

            def one_hots(c, u):
                for j in range(NEIGH):
                    last = pool.tensor_scalar(onehot[:, j, :], idx_in[u][:, :], pos[0:CTX, j:j + 1], None, ALU.is_equal)
                last.then_inc(onehot_done, 1)

            def gathers_over(c):
                wait(pool, pe_vg, 2, c, 2)

            def root1(c):
                wait(pool, ms1_done, 1, c, 1)
                pool.tensor_tensor(ms1_eps[:, :], ms1[:, :], eps1[:, :], ALU.add).then_inc(ms1_eps_done, 1)
                wait(pool, ms1_eps_done, 1, c, 1)
                pool.tensor_tensor(rs1[:, :], ms1_eps[:, :], half[:, 0:2], ALU.pow).then_inc(rs1_done, 1)

            def normalise(b, g):
                wait(pool, rsum_done, NG, b, g + 1)
                p = probs[g % 4][:, :, :]
                pool.tensor_tensor(p, p, rsum[:, g % 4, :].unsqueeze(2).broadcast_to([P, HG, CTX]),
                                   ALU.mult).then_inc(norm_done, 1)

            def w1o_low():
                pool.wait_ge(w1o_hi_done, 1)
                pool.tensor_tensor(w1o_lo[:, :, :], w1o_stage, w1o_hi[:, :, :].bitcast(F32), ALU.subtract).then_inc(w1o_done, 1)

            pool.wait_ge(pos_done, 1)
            split_xT(0, 0)
            split_ctxT(0, 0)
            root0(0, 0)
            one_hots(0, 0)

            def slot(s, u, kind):
                front, back, more = kind < NB, kind >= 1, kind < NB - 1
                b = s - 1
                if back:
                    normalise(b, 0)
                    normalise(b, 1)
                    normalise(b, 2)
                    normalise(b, 3)
                    normalise(b, 4)
                if more:
                    root0(s + 1, 1 - u, kind)
                if back:
                    normalise(b, 5)
                if more:
                    gathers_over(s)
                if back:
                    normalise(b, 6)
                if more:
                    one_hots(s + 1, 1 - u)
                if back:
                    normalise(b, 7)
                if front:
                    root1(s)
                if more:
                    split_ctxT(s + 1, 1 - u)
                    split_xT(s + 1, 1 - u)

            slots(pool, slot)

        @block.scalar
        def _(act):
            def squares(c, u, kind=None):
                wait_inputs(act, c, u)
                wait(act, rs_done, 1, c, 0)
                for t in range(TT):
                    act.activation(junk[:, t, :], x_in[u][:, t, :], ACT.Square, scale=ROOT, accum_out=ms[u][:, t:t + 1])
                act.activation(junk[0:CTX, 2, :], ctx_in[u][:, :], ACT.Square, scale=ROOT,
                               accum_out=ms[u][0:CTX, 2:3]).then_inc(ms_done, 1)
                if kind == 0:
                    act.wait_ge(w1o_in, 16)
                    act.activation(w1o_hi[:, :, :], w1o_stage, ACT.Copy).then_inc(w1o_hi_done, 1)

            def layer0_q(c, u):
                wait(act, pe_q0, 1, c, 1)
                wait(act, rs_done, 1, c, 1)
                wait(act, kprod_done, 2, c, 0)
                for t in range(TT):
                    last = act.activation(q0[:, t, :], g_ps[:, t * D:(t + 1) * D], ACT.Copy,
                                          scale=rs[u][:, t:t + 1])
                last.then_inc(q0_done, 1)

            def kv_high(c, u, kind):
                wait(act, pe_kv0, 1, c, 1)
                wait(act, rs_done, 1, c, 1)
                wait(act, pe_vg, 2, c, 0)
                act.activation(kv_hi[:, :, :].rearrange("p a n -> p (a n)"), turn_ps[BANK["kv0"]][0:CTX, :], ACT.Copy,
                               scale=rs[u][0:CTX, 2:3]).then_inc(kv_hi_done, 1)
                if kind == 0:
                    more_weights()

            def out_high(c):
                wait(act, pe_oT, 1, c, 1)
                wait(act, pe_q, 4, c - 1, 4)
                act.activation(oT_hi[:, :, :].rearrange("p a n -> p (a n)"), turn_ps[BANK["oT"]][:, :],
                               ACT.Copy).then_inc(oT_hi_done, 1)

            def squares1(c, u):
                wait(act, x1_done, 1, c, 1)
                wait(act, rs1_done, 1, c, 0)
                for t in range(TT):
                    last = act.activation(junk[:, 3 + t, :], x1[u][:, t, :], ACT.Square, scale=ROOT, accum_out=ms1[:, t:t + 1])
                last.then_inc(ms1_done, 1)

            def normed1(c, u):
                wait(act, rs1_done, 1, c, 1)
                wait(act, pe_oT, 1, c, 1)
                for t in range(TT):
                    last = act.activation(x1n[:, t, :], x1[u][:, t, :], ACT.Copy, scale=rs1[:, t:t + 1])
                last.then_inc(x1n_done, 1)

            def x1T_high(c):
                wait(act, pe_xT, 1, c, 1)
                wait(act, pe_oW, 1, c, 1)
                act.activation(x1T_hi[:, :, :].rearrange("p a n -> p (a n)"), turn_ps[BANK["xT"]][:, :],
                               ACT.Copy).then_inc(x1T_hi_done, 1)

            def k_high(c, k):
                wait(act, pe_k, 2, c, k + 1)
                wait(act, pe_s, NG, c - 1, NG)
                src = g_ps[:, k * 512:k * 512 + 4 * CTX].rearrange("p (c n) -> p c n", c=4)
                for h in range(2):
                    rows = slice(h * HD1, (h + 1) * HD1)
                    last = act.activation(k_hi[rows, 4 * k:4 * k + 4, h * CTX:(h + 1) * CTX], src[rows], ACT.Copy)
                last.then_inc(k_hi_done, 1)

            def v_copy(c, u, k):
                wait(act, pe_v, 2, c, k + 1)
                wait(act, pe_c, NHG, c - 1, 0)
                act.activation(v_sb[0:CTX, u, k * 512:(k + 1) * 512], turn_ps[BANK[f"v_{k}"]][0:CTX, :],
                               ACT.Copy).then_inc(v_done, 1)

            def q_high(b, k):
                wait(act, pe_q, 4, b, k + 1)
                wait(act, pe_s, NG, b, 2 * k - 2)
                act.activation(q_hi[k % 2][:, :, :].rearrange("p a n -> p (a n)"), turn_ps[BANK[f"q_{k}"]][:, :],
                               ACT.Copy).then_inc(q_hi_done, 1)

            def exponentials(b, g):
                wait(act, max_done, NG, b, g + 1)
                wait(act, pe_pT, NG, b, g - 3)
                for h in range(HG):
                    last = act.activation(probs[g % 4][:, h, :], score_ps[g % 2][:, h * CTX:(h + 1) * CTX], ACT.Exp,
                                          bias=neg_max[:, g % 4, h:h + 1], accum_out=sums[:, g % 4, h:h + 1])
                last.then_inc(exp_done, 1)

            def pT_copy(b, g):
                hg, t = g // 2, g % 2
                wait(act, pe_pT, NG, b, g + 1)
                wait(act, pe_c, NHG, b, hg - 1)
                act.activation(pT_sb[0:CTX, hg % 2, :, t * P:(t + 1) * P],
                               pT_ps[0:CTX, :].rearrange("p (h n) -> p h n", h=HG), ACT.Copy).then_inc(pT_done, 1)

            def c_high(b, hg):
                wait(act, pe_c, NHG, b, hg + 1)
                wait(act, pe_w, 2, b, 0)
                act.activation(c_hi[:, 2 * hg:2 * hg + 2, :].rearrange("p a n -> p (a n)"), c_ps[:, :],
                               ACT.Copy).then_inc(c_hi_done, 1)

            def small_high(n, dst, g=None):
                act.wait_ge(small_in[n], 16)
                for ch in range(DC):
                    scale = 1.0 if g is None else gamma[:, g, ch:ch + 1]
                    last = act.activation(dst[:, ch], small_stage[n][:, ch, :], ACT.Copy, scale=scale)
                last.then_inc(small_hi, 1)

            act.wait_ge(gamma_scaled, 1)
            small_high(0, w0q_hi[:, :, :], 0)
            act.wait_ge(ms_set, 1)
            squares(0, 0)
            small_high(1, w0kv_hi[:, :, 0, :], 1)
            small_high(2, w0kv_hi[:, :, 1, :], 1)
            act.wait_ge(w1v_in, 16)
            act.activation(w1v_hi[:, :, :], w1v_stage, ACT.Copy).then_inc(w1v_hi_done, 1)

            def more_weights():
                small_high(3, w0o_hi[:, :, :])
                act.wait_ge(w1q_in, 16)
                for ch in range(DC):
                    last = act.activation(w1q_hi[:, ch, :], w1q_stage[:, ch, :], ACT.Copy, scale=gamma[:, 2, ch:ch + 1])
                last.then_inc(w1q_hi_done, 1)
                act.wait_ge(k_zeroed, 1)

            def slot(s, u, kind):
                front, back, more = kind < NB, kind >= 1, kind < NB - 1
                b = s - 1
                if back:
                    q_high(b, 1)
                    exponentials(b, 0)
                if front:
                    layer0_q(s, u)
                if back:
                    exponentials(b, 1)
                if front:
                    kv_high(s, u, kind)
                if more:
                    squares(s + 1, 1 - u, kind)
                if back:
                    pT_copy(b, 0)
                    exponentials(b, 2)
                    q_high(b, 2)
                    pT_copy(b, 1)
                    exponentials(b, 3)
                    c_high(b, 0)
                    pT_copy(b, 2)
                    exponentials(b, 4)
                    q_high(b, 3)
                    pT_copy(b, 3)
                if front:
                    v_copy(s, u, 0)
                if back:
                    pT_copy(b, 4)
                    exponentials(b, 5)
                    c_high(b, 1)
                    exponentials(b, 6)
                    pT_copy(b, 5)
                if front:
                    out_high(s)
                    v_copy(s, u, 1)
                if back:
                    exponentials(b, 7)
                    c_high(b, 2)
                    pT_copy(b, 6)
                if front:
                    squares1(s, u)
                    k_high(s, 0)
                    normed1(s, u)
                if back:
                    pT_copy(b, 7)
                if front:
                    x1T_high(s)
                if back:
                    c_high(b, 3)
                if front:
                    q_high(s, 0)
                    k_high(s, 1)

            slots(act, slot)

        @block.vector
        def _(dve):
            def ctxT_high(c, u):
                wait_inputs(dve, c, u)
                wait(dve, pe_v, 2, c, 0)
                dve.tensor_copy(cT_hi[:, :, :], ctxT_in[u][:, :, :]).then_inc(cT_hi_done, 1)

            def xT_high(c, u):
                wait_inputs(dve, c, u)
                wait(dve, pe_q0, 1, c, 0)
                dve.tensor_copy(xT_hi[:, :, :], xT_in[u][:, :, :]).then_inc(xT_hi_done, 1)

            def kv_low(c, u, kind):
                wait(dve, kv_hi_done, 1, c, 1)
                dve.scalar_tensor_tensor(out=kv_lo[:, :, :].rearrange("p a n -> p (a n)"), in0=turn_ps[BANK["kv0"]][0:CTX, :],
                                         scalar=rs[u][0:CTX, 2:3],
                                         in1=kv_hi[:, :, :].rearrange("p a n -> p (a n)").bitcast(F32),
                                         op0=ALU.mult, op1=ALU.subtract).then_inc(kv_done, 1)
                if kind == 0:
                    small_low(3, w0o_hi[:, :, :], w0o_lo[:, :, :])

            def low(dst, hi, src, hi_done, per, batch, n, done):
                wait(dve, hi_done, per, batch, n)
                dve.tensor_tensor(dst, src, hi.bitcast(F32), ALU.subtract).then_inc(done, 1)

            def key_products0(c, t):
                wait(dve, o0_done, 2, c - 1, t + 1)
                wait(dve, pe_kg, 2, c, t + 1)
                wait(dve, q0_done, 1, c, 1)
                dve.tensor_tensor(prod[t][:, :].rearrange("p (j d) -> p j d", j=NEIGH),
                                  g_ps[:, 0:NEIGH * D].rearrange("p (j d) -> p j d", j=NEIGH),
                                  q0[:, t, :].unsqueeze(1).broadcast_to([P, NEIGH, D]), ALU.mult).then_inc(kprod_done, 1)

            def key_sums0(c, t):
                wait(dve, kprod_done, 2, c, t + 1)
                dve.tensor_reduce(s0[:, t, :, :].rearrange("p j h -> p (j h)"),
                                  prod[t][:, :].rearrange("p (a e) -> p a e", e=HD0), X_AXIS, ALU.add).then_inc(score0_done, 1)

            def weights_squared(c):
                wait(dve, score0_done, 2, c, 2)
                flat = lambda a: a[:, :, :, :].rearrange("p t j h -> p (t j h)")
                dve.scalar_tensor_tensor(out=flat(w0), in0=flat(s0), scalar=0.0, in1=flat(s0),
                                         op0=ALU.max, op1=ALU.mult).then_inc(weight_steps, 1)

            def weights_summed(c):
                wait(dve, weight_steps, 4, c, 1)
                dve.tensor_reduce(den[:, :, :], w0[:, :, :, :].rearrange("p t j h -> p t h j"), X_AXIS,
                                  ALU.add).then_inc(weight_steps, 1)

            def weights_guarded(c):
                wait(dve, weight_steps, 4, c, 2)
                dve.tensor_scalar(den_c[:, :, :], den[:, :, :], EPS_DEN, None, ALU.max).then_inc(weight_steps, 1)

            def weights_inverted(c):
                wait(dve, weight_steps, 4, c, 3)
                dve.reciprocal(rden[:, :, :], den_c[:, :, :]).then_inc(weight_steps, 1)

            def weights_normed(c):
                wait(dve, weight_steps, 4, c, 4)
                dve.tensor_tensor(wn[:, :, :, :], w0[:, :, :, :],
                                  rden[:, :, :].unsqueeze(2).broadcast_to([P, TT, NEIGH, H0]), ALU.mult).then_inc(weights_done, 1)

            def value_products0(c, t):
                wait(dve, pe_vg, 2, c, t + 1)
                wait(dve, weights_done, 1, c, 1)
                dve.tensor_tensor(prod[t][:, :].rearrange("p (a e) -> p a e", e=HD0),
                                  g_ps[:, 0:NEIGH * D].rearrange("p (a e) -> p a e", e=HD0),
                                  wn[:, t, :, :].rearrange("p j h -> p (j h)").unsqueeze(2).broadcast_to([P, NEIGH * H0, HD0]),
                                  ALU.mult).then_inc(vprod_done, 1)

            def pair_sum0(c, t):
                wait(dve, vprod_done, 2, c, t + 1)
                dve.tensor_tensor(prod[t][:, 0:D], prod[t][:, 0:D], prod[t][:, D:2 * D], ALU.add).then_inc(pair_sum_done, 1)

            def value_sum0(c, t):
                wait(dve, pair_sum_done, 2, c, t + 1)
                if t == 0:
                    wait(dve, pe_xT, 1, c, 0)
                dve.tensor_tensor(o0[:, t, :], prod[t][:, 0:D], prod[t][:, 2 * D:3 * D], ALU.add).then_inc(o0_done, 1)

            def out_low(c):
                low(oT_lo[:, :, :].rearrange("p a n -> p (a n)"), oT_hi[:, :, :].rearrange("p a n -> p (a n)"),
                    turn_ps[BANK["oT"]][:, :], oT_hi_done, 1, c, 1, oT_done)

            def x1T_low(c):
                low(x1T_lo[:, :, :].rearrange("p a n -> p (a n)"), x1T_hi[:, :, :].rearrange("p a n -> p (a n)"),
                    turn_ps[BANK["xT"]][:, :], x1T_hi_done, 1, c, 1, x1T_done)

            def residual0(c, u, kind):
                wait(dve, pe_oW, 1, c, 1)
                wait_inputs(dve, c, u)
                dve.tensor_tensor(x1[u][:, :, :].rearrange("p t d -> p (t d)"), turn_ps[BANK["oW"]][:, :],
                                  x_in[u][:, :, :].rearrange("p t d -> p (t d)"), ALU.add).then_inc(x1_done, 1)
                if kind == 0:
                    w1q_low()

            def k_low(c, k):
                wait(dve, k_hi_done, 2, c, k + 1)
                src = g_ps[:, k * 512:k * 512 + 4 * CTX].rearrange("p (c n) -> p c n", c=4)
                for h in range(2):
                    rows = slice(h * HD1, (h + 1) * HD1)
                    at = (rows, slice(4 * k, 4 * k + 4), slice(h * CTX, (h + 1) * CTX))
                    last = dve.tensor_tensor(k_lo[at], src[rows], k_hi[at].bitcast(F32), ALU.subtract)
                last.then_inc(k_done, 1)

            def q_low(b, k):
                low(q_lo[k % 2][:, :, :].rearrange("p a n -> p (a n)"), q_hi[k % 2][:, :, :].rearrange("p a n -> p (a n)"),
                    turn_ps[BANK[f"q_{k}"]][:, :], q_hi_done, 4, b, k + 1, q_done)

            def c_low(b, hg):
                low(c_lo[:, 2 * hg:2 * hg + 2, :].rearrange("p a n -> p (a n)"),
                    c_hi[:, 2 * hg:2 * hg + 2, :].rearrange("p a n -> p (a n)"), c_ps[:, :], c_hi_done, NHG, b, hg + 1, c_done)

            def maxima(b, g):
                wait(dve, pe_s, NG, b, g + 1)
                view = score_ps[g % 2][:, 0:GC].rearrange("p (h n) -> p h n", h=HG)
                dve.tensor_reduce(neg_max[:, g % 4, :], view, X_AXIS, ALU.max, negate=True).then_inc(max_done, 1)

            def recip(b, g):
                wait(dve, exp_done, NG, b, g + 1)
                dve.reciprocal(rsum[:, g % 4, :], sums[:, g % 4, :]).then_inc(rsum_done, 1)

            def result(b, u, t):
                wait(dve, pe_w, 2, b, t + 1)
                if t == 0:
                    wait(dve, y_out, 16, b, 0)
                dve.tensor_tensor(y[:, t, :], turn_ps[BANK[f"w{t}"]][:, 0:D], x1[u][:, t, :], ALU.add).then_inc(y_done, 1)

            dve.wait_ge(gamma_in, 16)
            dve.tensor_scalar(gamma[:, 0, :], gamma[:, 0, :], HD0 ** -0.5, None, ALU.mult).then_inc(gamma_scaled, 1)
            for u in range(2):
                last = dve.memset(ms[u][:, :], 1.0)
            last.then_inc(ms_set, 1)
            dve.wait_ge(const_steps, 5)
            dve.tensor_copy(pos[:, :], pos_i[:, :]).then_inc(pos_done, 1)
            dve.memset(k_hi[:, :, :].bitcast(F32), 0.0)

            def small_low(n, hi, lo, g=None):
                dve.wait_ge(small_hi, n + 1)
                for ch in range(DC):
                    scale = 1.0 if g is None else gamma[:, g, ch:ch + 1]
                    last = dve.scalar_tensor_tensor(out=lo[:, ch], in0=small_stage[n][:, ch, :], scalar=scale,
                                                    in1=hi[:, ch].bitcast(F32), op0=ALU.mult, op1=ALU.subtract)
                last.then_inc(small_split, 1)

            dve.wait_ge(gamma_scaled, 1)
            xT_high(0, 0)
            ctxT_high(0, 0)
            small_low(0, w0q_hi[:, :, :], w0q_lo[:, :, :], 0)
            small_low(1, w0kv_hi[:, :, 0, :], w0kv_lo[:, :, 0, :], 1)
            small_low(2, w0kv_hi[:, :, 1, :], w0kv_lo[:, :, 1, :], 1)
            dve.memset(k_lo[:, :, :].bitcast(F32), 0.0).then_inc(k_zeroed, 1)
            dve.wait_ge(w1v_hi_done, 1)
            dve.tensor_tensor(w1v_lo[:, :, :], w1v_stage, w1v_hi[:, :, :].bitcast(F32), ALU.subtract).then_inc(w1v_done, 1)

            def w1q_low():
                dve.wait_ge(w1q_hi_done, 1)
                for ch in range(DC):
                    last = dve.scalar_tensor_tensor(out=w1q_lo[:, ch, :], in0=w1q_stage[:, ch, :], scalar=gamma[:, 2, ch:ch + 1],
                                                    in1=w1q_hi[:, ch, :].bitcast(F32), op0=ALU.mult, op1=ALU.subtract)
                last.then_inc(w1q_done, 1)

            def slot(s, u, kind):
                front, back, older, more = kind < NB, kind >= 1, kind >= 2, kind < NB - 1
                b = s - 1
                if back:
                    maxima(b, 0)
                    q_low(b, 1)
                    maxima(b, 1)
                    recip(b, 0)
                if older:
                    result(s - 2, u, 1)
                if back:
                    recip(b, 1)
                if front:
                    kv_low(s, u, kind)
                if back:
                    maxima(b, 2)
                if front:
                    key_products0(s, 0)
                    key_sums0(s, 0)
                if back:
                    recip(b, 2)
                    maxima(b, 3)
                    q_low(b, 2)
                if front:
                    key_products0(s, 1)
                    key_sums0(s, 1)
                if back:
                    maxima(b, 4)
                if front:
                    weights_squared(s)
                    weights_summed(s)
                if back:
                    recip(b, 3)
                if front:
                    weights_guarded(s)
                    weights_inverted(s)
                    weights_normed(s)
                if back:
                    recip(b, 4)
                    maxima(b, 5)
                if front:
                    value_products0(s, 0)
                if back:
                    q_low(b, 3)
                if front:
                    pair_sum0(s, 0)
                if back:
                    c_low(b, 0)
                if front:
                    value_sum0(s, 0)
                    value_products0(s, 1)
                if back:
                    recip(b, 5)
                    maxima(b, 6)
                if front:
                    pair_sum0(s, 1)
                    value_sum0(s, 1)
                if back:
                    c_low(b, 1)
                if more:
                    xT_high(s + 1, 1 - u)
                if back:
                    recip(b, 6)
                if front:
                    out_low(s)
                if back:
                    maxima(b, 7)
                    recip(b, 7)
                if front:
                    residual0(s, u, kind)
                if back:
                    c_low(b, 2)
                if more:
                    ctxT_high(s + 1, 1 - u)
                if front:
                    x1T_low(s)
                if back:
                    c_low(b, 3)
                if front:
                    k_low(s, 0)
                    q_low(s, 0)
                if back:
                    result(b, 1 - u, 0)
                if front:
                    k_low(s, 1)

            slots(dve, slot)
            result(NB - 1, 1, 1)

        @block.tensor
        def _(pe):
            def take_bank(name, s, kind):
                before = turn_before(name, kind)
                if before:
                    name_before, rel = before
                    done, per, n = EMPTIED[name_before]
                    wait(pe, done, per, s + rel, n)
                return turn_ps[BANK[name]]

            def split_product(dst, pairs):
                todo = [(a, b) for (a_hi, a_lo), (b_hi, b_lo) in pairs
                        for a, b in ((a_hi, b_hi), (a_hi, b_lo), (a_lo, b_hi))]
                for n, (a, b) in enumerate(todo):
                    last = pe.matmul(dst, a, b, start=n == 0, stop=n == len(todo) - 1)
                return last

            def layer0_q(c):
                wait(pe, k_done, 2, c, -1)
                wait(pe, xT_done, 1, c, 1)
                for t in range(TT):
                    rows = slice(t * P, (t + 1) * P)
                    last = split_product(g_ps[:, t * D:(t + 1) * D],
                                         [((xT_hi[:, ch, rows], xT_lo[:, ch, rows]), (w0q_hi[:, ch, :], w0q_lo[:, ch, :]))
                                          for ch in range(DC)])
                last.then_inc(pe_q0, 1)

            def layer0_kv(c, kind):
                if kind == 0:
                    pe.wait_ge(small_split, 3)
                bank = take_bank("kv0", c, kind)
                wait(pe, cT_done, 1, c, 1)
                split_product(bank[0:CTX, :],
                              [((cT_hi[:, ch, :], cT_lo[:, ch, :]),
                                (w0kv_hi[:, ch, :, :].rearrange("p a n -> p (a n)"), w0kv_lo[:, ch, :, :].rearrange("p a n -> p (a n)")))
                               for ch in range(DC)]).then_inc(pe_kv0, 1)

            def gather(c, t, part, done):
                for j in range(NEIGH):
                    for n, kv in enumerate((kv_hi, kv_lo)):
                        last = pe.matmul(g_ps[:, j * D:(j + 1) * D], onehot[:, j, t * P:(t + 1) * P], kv[:, part, :],
                                         start=n == 0, stop=n == 1)
                last.then_inc(done, 1)

            def gather_k(c, t):
                if t == 0:
                    wait(pe, kv_done, 1, c, 1)
                    wait(pe, onehot_done, 1, c, 1)
                    wait(pe, q0_done, 1, c, 1)
                    wait(pe, k_done, 2, c, 0)
                else:
                    wait(pe, kprod_done, 2, c, 1)
                gather(c, t, 0, pe_kg)

            def gather_v(c, t):
                if t == 0:
                    wait(pe, kprod_done, 2, c, 2)
                else:
                    wait(pe, vprod_done, 2, c, 1)
                gather(c, t, 1, pe_vg)

            def transposes(bank, src, done):
                for ch in range(DC):
                    for t in range(TT):
                        last = pe.transpose(bank[:, ch * T + t * P:ch * T + (t + 1) * P], src[:, t, ch * P:(ch + 1) * P], ident[:, :])
                last.then_inc(done, 1)

            def out_transposed(c, kind):
                bank = take_bank("oT", c, kind)
                wait(pe, o0_done, 2, c, 2)
                transposes(bank, o0, pe_oT)

            def out_product(c, kind):
                if kind == 0:
                    pe.wait_ge(small_split, 4)
                bank = take_bank("oW", c, kind)
                wait(pe, oT_done, 1, c, 1)
                for t in range(TT):
                    rows = slice(t * P, (t + 1) * P)
                    last = split_product(bank[:, t * D:(t + 1) * D],
                                         [((oT_hi[:, ch, rows], oT_lo[:, ch, rows]), (w0o_hi[:, ch, :], w0o_lo[:, ch, :]))
                                          for ch in range(DC)])
                last.then_inc(pe_oW, 1)

            def x1_transposed(c, kind):
                bank = take_bank("xT", c, kind)
                wait(pe, x1n_done, 1, c, 1)
                transposes(bank, x1n, pe_xT)

            def keys(c, u, k, kind):
                if kind == 0 and k == 0:
                    pe.wait_ge(w1k_in, 16)
                wait(pe, vprod_done, 2, c, 2)
                wait_inputs(pe, c, u)
                bank = g_ps[:, k * 512:(k + 1) * 512]
                for n in range(4):
                    cols = slice((4 * k + n) * P, (4 * k + n + 1) * P)
                    for ch in range(DC):
                        last = pe.matmul(bank[:, n * CTX:(n + 1) * CTX], w1k_sb[:, ch, cols], ctxT_in[u][:, ch, :],
                                         start=ch == 0, stop=ch == DC - 1)
                last.then_inc(pe_k, 1)

            def values(c, k, kind):
                if kind == 0 and k == 0:
                    pe.wait_ge(w1v_done, 1)
                bank = take_bank(f"v_{k}", c, kind)
                wait(pe, cT_done, 1, c, 1)
                cols = slice(k * 512, (k + 1) * 512)
                split_product(bank[0:CTX, :], [((cT_hi[:, ch, :], cT_lo[:, ch, :]), (w1v_hi[:, ch, cols], w1v_lo[:, ch, cols]))
                                               for ch in range(DC)]).then_inc(pe_v, 1)

            def queries(b, s, k, kind):
                if kind == 0:
                    pe.wait_ge(w1q_done, 1)
                bank = take_bank(f"q_{k}", s, kind)
                wait(pe, x1T_done, 1, b, 1)
                for n in range(2):
                    cols = slice((2 * k + n) * P, (2 * k + n + 1) * P)
                    last = split_product(bank[:, n * T:(n + 1) * T],
                                         [((w1q_hi[:, ch, cols], w1q_lo[:, ch, cols]), (x1T_hi[:, ch, :], x1T_lo[:, ch, :]))
                                          for ch in range(DC)])
                last.then_inc(pe_q, 1)

            def scores(b, g):
                hg, t = g // 2, g % 2
                if t == 0:
                    wait(pe, q_done, 4, b, hg + 1)
                    if hg % 2 == 0:
                        wait(pe, k_done, 2, b, hg // 2 + 1)
                before, batch = (g - 2, b) if g >= 2 else (g + 6, b - 1)
                wait(pe, exp_done, NG, batch, before + 1)
                for n in range(2):
                    pair, rows = 2 * hg + n, slice(t * P, (t + 1) * P)
                    last = split_product(score_ps[g % 2][:, n * 2 * CTX:(n + 1) * 2 * CTX],
                                         [((q_hi[hg % 2][:, n, rows], q_lo[hg % 2][:, n, rows]), (k_hi[:, pair, :], k_lo[:, pair, :]))])
                last.then_inc(pe_s, 1)

            def probs_transposed(b, g):
                wait(pe, norm_done, NG, b, g + 1)
                wait(pe, pT_done, NG, b, g)
                for h in range(HG):
                    last = pe.transpose(pT_ps[0:CTX, h * P:(h + 1) * P], probs[g % 4][:, h, :], ident[:, :])
                last.then_inc(pe_pT, 1)

            def mix(b, u, hg):
                wait(pe, pT_done, NG, b, 2 * hg + 2)
                if hg % 2 == 0:
                    wait(pe, v_done, 2, b, hg // 2 + 1)
                wait(pe, c_done, NHG, b, hg)
                for n in range(2):
                    for h in range(2):
                        head = 4 * hg + 2 * n + h
                        last = pe.matmul(c_ps[h * HD1:(h + 1) * HD1, n * T:(n + 1) * T],
                                         v_sb[0:CTX, u, head * HD1:(head + 1) * HD1],
                                         pT_sb[0:CTX, hg % 2, 2 * n + h, :], start=True, stop=True)
                last.then_inc(pe_c, 1)

            def output(b, t, first, end, kind):
                bank = take_bank(f"w{t}", b + 2 if t else b + 1, kind) if first == 0 else turn_ps[BANK[f"w{t}"]]
                if kind == 1 and first == 0:
                    pe.wait_ge(w1o_done, 1)
                wait(pe, c_done, NHG, b, end // 2)
                rows = slice(t * P, (t + 1) * P)
                todo = [(a, w) for ch in range(first, end)
                        for a, w in ((c_hi[:, ch, rows], w1o_hi[:, ch, :]), (c_hi[:, ch, rows], w1o_lo[:, ch, :]),
                                     (c_lo[:, ch, rows], w1o_hi[:, ch, :]))]
                for n, (a, w) in enumerate(todo):
                    last = pe.matmul(bank[:, 0:D], a, w, start=first == 0 and n == 0,
                                     stop=end == EC and n == len(todo) - 1)
                if end == EC:
                    last.then_inc(pe_w, 1)

            pe.wait_ge(const_done, 1)
            pe.wait_ge(small_split, 1)

            def slot(s, u, kind):
                front, back, older = kind < NB, kind >= 1, kind >= 2
                b = s - 1
                if front:
                    layer0_q(s)
                if back:
                    scores(b, 0)
                    queries(b, s, 1, kind)
                if older:
                    output(s - 2, 1, 0, 2, kind)
                if back:
                    scores(b, 1)
                if older:
                    output(s - 2, 1, 2, 4, kind)
                    output(s - 2, 1, 4, 6, kind)
                    output(s - 2, 1, 6, EC, kind)
                if front:
                    layer0_kv(s, kind)
                if back:
                    scores(b, 2)
                    probs_transposed(b, 0)
                if front:
                    values(s, 0, kind)
                    gather_k(s, 0)
                if back:
                    queries(b, s, 2, kind)
                    scores(b, 3)
                    probs_transposed(b, 1)
                if front:
                    gather_k(s, 1)
                if back:
                    mix(b, 1 - u, 0)
                    probs_transposed(b, 2)
                    scores(b, 4)
                    scores(b, 5)
                if front:
                    gather_v(s, 0)
                if back:
                    queries(b, s, 3, kind)
                    probs_transposed(b, 3)
                    probs_transposed(b, 4)
                if front:
                    gather_v(s, 1)
                if back:
                    scores(b, 6)
                    mix(b, 1 - u, 1)
                if front:
                    values(s, 1, kind)
                if back:
                    probs_transposed(b, 5)
                if front:
                    out_transposed(s, kind)
                if back:
                    scores(b, 7)
                    mix(b, 1 - u, 2)
                    probs_transposed(b, 6)
                if front:
                    out_product(s, kind)
                    keys(s, u, 0, kind)
                if back:
                    output(b, 0, 0, 2, kind)
                    output(b, 0, 2, 4, kind)
                    probs_transposed(b, 7)
                    output(b, 0, 4, 6, kind)
                if front:
                    x1_transposed(s, kind)
                if back:
                    mix(b, 1 - u, 3)
                if front:
                    keys(s, u, 1, kind)
                    queries(s, s, 0, kind)
                if back:
                    output(b, 0, 6, EC, kind)

            slots(pe, slot)
            output(NB - 1, 1, 0, EC, NB + 1)


def kernel(x, ctx_1024, itok_BxS_0_255, L0_xattn_gamma_q, L0_xattn_gamma_kv, L0_xattn_Wq, L0_xattn_Wk, L0_xattn_Wv,
           L0_xattn_Wo, L1_xattn_wq, L1_xattn_wk, L1_xattn_wv, L1_xattn_wo, L1_xattn_norm_w):
    import numpy as np
    import concourse.bacc as bacc
    from concourse.bass_utils import run_bass_kernel_spmd

    turned = lambda a, *axes: np.ascontiguousarray(np.transpose(np.asarray(a), axes))
    plain = lambda a: np.ascontiguousarray(np.asarray(a))
    arrays = {
        "x": plain(x), "xT": turned(x, 0, 2, 1), "ctx": plain(ctx_1024), "ctxT": turned(ctx_1024, 0, 2, 1),
        "idx": plain(itok_BxS_0_255), 
        "gammas": turned(np.stack([plain(g).reshape(DC, P) for g in
                                   (L0_xattn_gamma_q, L0_xattn_gamma_kv, L1_xattn_norm_w)]), 2, 0, 1),
        "w0qT": turned(L0_xattn_Wq, 1, 0), "w0kT": turned(L0_xattn_Wk, 1, 0), "w0vT": turned(L0_xattn_Wv, 1, 0),
        "w0oT": turned(L0_xattn_Wo, 1, 0), "w1q": plain(L1_xattn_wq), "w1k": plain(L1_xattn_wk),
        "w1v": plain(L1_xattn_wv), "w1o": plain(L1_xattn_wo),
    }
    nc = bacc.Bacc("TRN2", target_bir_lowering=False, num_devices=1)
    aps = {n: nc.dram_tensor(f"in_{n}", a.shape, mybir.dt.from_np(a.dtype), kind="ExternalInput").ap()
           for n, a in arrays.items()}
    out = nc.dram_tensor("out", (NB, T, D), F32, kind="ExternalOutput").ap()
    build(nc, **aps, out=out)
    r = run_bass_kernel_spmd(nc, [{f"in_{n}": a for n, a in arrays.items()}], core_ids=[0])
    return r.results[0]["out"]
```
